# Optimizing a Trainium2 kernel written in Bass

```python
import numpy as np
import jax
import jax.numpy as jnp

def _softmax(x, axis=-1):
    return jax.nn.softmax(x, axis=axis)

def _gelu(x):
    return jax.nn.gelu(x, approximate=True)

def _silu(x):
    return jax.nn.silu(x)

def _sigmoid(x):
    return jax.nn.sigmoid(x)

def _layernorm(x, axis=-1, eps=1e-05):
    m = jnp.mean(x, axis=axis, keepdims=True)
    v = jnp.var(x, axis=axis, keepdims=True)
    return (x - m) / jnp.sqrt(v + eps)

def _scatter_add(tgt, idx, src, axis=0):
    return tgt.at[idx].add(src)

def _segment_sum(src, seg, n):
    return jax.ops.segment_sum(src, seg, n)
kernel_name = 'mk_decoder_postln_d1_seqx_r8_070c0b'

def setup_inputs(seed: int=0):
    np.random.seed(seed)
    _w = jnp.asarray

    def _rec_inputs():
        import jax
        import jax.numpy as jnp
        _rk = jax.random.key(seed)
        x = -0.0002928 + 1 * jax.random.normal(jax.random.fold_in(_rk, 1), (4, 256, 128), jnp.float32)
        _lenS = 256 - jax.random.randint(jax.random.fold_in(_rk, 7), (4,), 0, max(1, 256 // 4) + 1, jnp.int32)
        _lenS2 = 64 - jax.random.randint(jax.random.fold_in(_rk, 8), (4,), 0, max(1, 64 // 4) + 1, jnp.int32)
        _ctx_512P = jax.random.normal(jax.random.fold_in(_rk, 11), (4, 16, 64), jnp.float32)
        _ctx_512c = jax.random.dirichlet(jax.random.fold_in(_rk, 511), 0.3 * jnp.ones((16,), jnp.float32), (4, 64))
        _ctx_512t = jnp.einsum('bsk,bkd->bsd', _ctx_512c, _ctx_512P)
        _ctx_512t = _ctx_512t * jax.lax.rsqrt(jnp.mean(jnp.square(_ctx_512t)) + 1e-12) * 0.953939
        ctx_512 = 0.00222621 + 0.99962 * (_ctx_512t + 0.3 * jax.random.normal(jax.random.fold_in(_rk, 611), (4, 64, 64), jnp.float32))
        return (x, ctx_512)
    x, ctx_512 = _rec_inputs()

    def _L0_attn_setup():
        import jax, jax.numpy as jnp
        import numpy as np
        B, T, C = (4, 128, 128)
        HEAD = 64
        H = C // HEAD
        LORA_MIX = 32
        LORA_DECAY = 64
        LN_EPS = 0.00064

        def _wkv6(r, k, v, w, u):
            rT = jnp.moveaxis(r, 1, 0)
            kT = jnp.moveaxis(k, 1, 0)
            vT = jnp.moveaxis(v, 1, 0)
            wT = jnp.moveaxis(w, 1, 0)

            def step(S, inputs):
                rt, kt, vt, wt = inputs
                kv = kt[..., :, None] * vt[..., None, :]
                y = jnp.einsum('bhi,bhij->bhj', rt, S + u[None, :, :, None] * kv)
                S = wt[..., :, None] * S + kv
                return (S, y)
            S0 = jnp.zeros((r.shape[0], H, HEAD, HEAD), r.dtype)
            _, yT = jax.lax.scan(step, S0, (rT, kT, vT, wT))
            return jnp.moveaxis(yT, 0, 1)

        def _tmix_forward(x, time_maa_x, time_maa_w, time_maa_k, time_maa_v, time_maa_r, time_maa_w1, time_maa_w2, time_decay, time_decay_w1, time_decay_w2, time_faaaa, W_r, W_k, W_v, W_o, ln_w, ln_b):
            b, t, c = x.shape
            xshift = jnp.pad(x, ((0, 0), (1, 0), (0, 0)))[:, :t]
            xx = xshift - x
            xxx = x + xx * time_maa_x
            m = jnp.tanh(xxx @ time_maa_w1).reshape(b, t, 4, LORA_MIX)
            m = jnp.einsum('btfl,flc->fbtc', m, time_maa_w2)
            mw, mk, mv, mr = (m[0], m[1], m[2], m[3])
            xw = x + xx * (time_maa_w + mw)
            xk = x + xx * (time_maa_k + mk)
            xv = x + xx * (time_maa_v + mv)
            xr = x + xx * (time_maa_r + mr)
            r = (xr @ W_r).reshape(b, t, H, HEAD)
            k = (xk @ W_k).reshape(b, t, H, HEAD)
            v = (xv @ W_v).reshape(b, t, H, HEAD)
            ww = time_decay + jnp.tanh(xw @ time_decay_w1) @ time_decay_w2
            w = jnp.exp(-jnp.exp(ww)).reshape(b, t, H, HEAD)
            y = _wkv6(r, k, v, w, time_faaaa)
            mean = y.mean(-1, keepdims=True)
            var = y.var(-1, keepdims=True)
            yn = ((y - mean) * jax.lax.rsqrt(var + LN_EPS)).reshape(b, t, c)
            yn = yn * ln_w + ln_b
            return yn @ W_o
        key0 = jax.random.key(seed)
        ks = jax.random.split(key0, 24)
        rn = lambda k, shape, s: jax.random.normal(k, shape, jnp.float32) * s
        inp = {'query': jax.random.normal(ks[0], (B, T, C), jnp.float32), 'key': jax.random.normal(ks[1], (B, T, C), jnp.float32), 'value': jax.random.normal(ks[2], (B, T, C), jnp.float32), 'time_maa_x': rn(ks[3], (C,), 0.1) + 0.5, 'time_maa_w': rn(ks[4], (C,), 0.1) + 0.5, 'time_maa_k': rn(ks[5], (C,), 0.1) + 0.5, 'time_maa_v': rn(ks[6], (C,), 0.1) + 0.5, 'time_maa_r': rn(ks[7], (C,), 0.1) + 0.5, 'time_maa_w1': rn(ks[8], (C, 4 * LORA_MIX), 0.02), 'time_maa_w2': rn(ks[9], (4, LORA_MIX, C), 0.02), 'time_decay': rn(ks[10], (C,), 0.5) - 5.0, 'time_decay_w1': rn(ks[11], (C, LORA_DECAY), 0.02), 'time_decay_w2': rn(ks[12], (LORA_DECAY, C), 0.02), 'time_faaaa': rn(ks[13], (H, HEAD), 0.5), 'W_r': rn(ks[14], (C, C), 0.02), 'W_k': rn(ks[15], (C, C), 0.02), 'W_v': rn(ks[16], (C, C), 0.02), 'W_o': rn(ks[17], (C, C), 0.02), 'ln_w': jnp.ones((C,), jnp.float32), 'ln_b': jnp.zeros((C,), jnp.float32)}
        return inp
    _L0_attn_all = _L0_attn_setup()
    _L0_attn_in = {k: v for k, v in _L0_attn_all.items() if k in ('key', 'value', 'time_maa_x', 'time_maa_w', 'time_maa_k', 'time_maa_v', 'time_maa_r', 'time_maa_w1', 'time_maa_w2', 'time_decay', 'time_decay_w1', 'time_decay_w2', 'time_faaaa', 'W_r', 'W_k', 'W_v', 'W_o', 'ln_w', 'ln_b')}
    del _L0_attn_all

    def _L0_xattn_setup():
        import jax, jax.numpy as jnp
        import numpy as np
        B, T, TC, C, CC, H = (2, 256, 64, 128, 64, 16)
        D = C // H

        def _heads(t):
            b, l, _ = t.shape
            return t.reshape(b, l, H, D).transpose(0, 2, 1, 3)
        key = jax.random.key(seed)
        ks = jax.random.split(key, 18)
        w = lambda k, i, o: jax.random.normal(k, (i, o), jnp.float32) / np.sqrt(i).astype(np.float32)
        return {'x': jax.random.normal(ks[0], (B, T, C), jnp.float32), 'cross_input': jax.random.normal(ks[1], (B, TC, CC), jnp.float32), 'Wk': w(ks[2], C, C), 'bk': jnp.zeros((C,), jnp.float32), 'Wq': w(ks[3], C, C), 'bq': jnp.zeros((C,), jnp.float32), 'Wv': w(ks[4], C, C), 'bv': jnp.zeros((C,), jnp.float32), 'Wck': w(ks[5], CC, C), 'bck': jnp.zeros((C,), jnp.float32), 'Wcq': w(ks[6], C, C), 'bcq': jnp.zeros((C,), jnp.float32), 'Wcv': w(ks[7], CC, C), 'bcv': jnp.zeros((C,), jnp.float32), 'Wp': w(ks[8], C, C), 'bp': jnp.zeros((C,), jnp.float32)}
    _L0_xattn_all = _L0_xattn_setup()
    _L0_xattn_in = {k: v for k, v in _L0_xattn_all.items() if k in ('Wk', 'bk', 'Wq', 'bq', 'Wv', 'bv', 'Wck', 'bck', 'Wcq', 'bcq', 'Wcv', 'bcv', 'Wp', 'bp')}
    del _L0_xattn_all

    def _L0_ffn_setup():
        import jax, jax.numpy as jnp
        import numpy as np
        DIM = 128
        DEPTH = 6
        HEADS = 16
        DIM_HEAD = 64
        WINDOW = 32
        INNER = HEADS * DIM_HEAD
        DIM_INNER = int(DIM * 4 * 2 / 3)
        QK_SCALE = 8.0

        def shift_tokens(t):
            a, s = jnp.split(t, 2, -1)
            s = jnp.pad(s, ((0, 0), (1, 0), (0, 0)))[:, :-1]
            return jnp.concatenate([a, s], -1)

        def l2norm(t):
            return t / jnp.maximum(jnp.linalg.norm(t, axis=-1, keepdims=True), 1e-12)

        def rotate_half(x):
            x1, x2 = jnp.split(x, 2, -1)
            return jnp.concatenate([-x2, x1], -1)

        def rotary_tables(n):
            half = jnp.arange(0, DIM_HEAD, 2, dtype=jnp.float32)
            inv_freq = 1.0 / 10000.0 ** (half / DIM_HEAD)
            t = jnp.arange(n, dtype=jnp.float32)
            freqs = t[:, None] * inv_freq[None, :]
            freqs = jnp.concatenate([freqs, freqs], -1)
            base_scale = (half + 0.4 * DIM_HEAD) / (1.4 * DIM_HEAD)
            power = (t - n // 2) / (WINDOW // 2)
            scale = base_scale[None, :] ** power[:, None]
            scale = jnp.concatenate([scale, scale], -1)
            return (freqs, scale)

        def local_attention(q, k, v):
            b, h, n, d = q.shape
            w = WINDOW
            nw = n // w
            bq = q.reshape(b, h, nw, w, d)
            bk = k.reshape(b, h, nw, w, d)
            bv = v.reshape(b, h, nw, w, d)

            def look(t):
                p = jnp.pad(t, ((0, 0), (0, 0), (1, 0), (0, 0), (0, 0)))
                return jnp.concatenate([p[:, :, :nw], p[:, :, 1:]], axis=3)
            bk2, bv2 = (look(bk), look(bv))
            seq = jnp.arange(n).reshape(nw, w)
            seq_p = jnp.pad(seq, ((1, 0), (0, 0)), constant_values=-1)
            jt = jnp.concatenate([seq_p[:nw], seq_p[1:]], axis=1)
            it = seq[:, :, None]
            jb = jt[:, None, :]
            mask = (it < jb) | (it > jb + w) | (jb == -1)
            sim = jnp.einsum('bhwie,bhwje->bhwij', bq, bk2) * QK_SCALE
            sim = jnp.where(mask, -jnp.finfo(sim.dtype).max, sim)
            attn = jax.nn.softmax(sim, -1)
            out = jnp.einsum('bhwij,bhwje->bhwie', attn, bv2)
            return out.reshape(b, h, n, d)

        def attn_layer(x, Wqkv, qs, ksc, Wo):
            b, n, _ = x.shape
            qkv = x @ Wqkv
            q, k, v = jnp.split(qkv, 3, -1)
            sh = lambda t: t.reshape(b, n, HEADS, DIM_HEAD).transpose(0, 2, 1, 3)
            q, k, v = (sh(q), sh(k), sh(v))
            q = l2norm(q) * qs
            k = l2norm(k) * ksc
            freqs, scale = rotary_tables(n)
            cos, sin = (jnp.cos(freqs), jnp.sin(freqs))
            q = q * cos * scale + rotate_half(q) * sin * scale
            inv = 1.0 / scale
            k = k * cos * inv + rotate_half(k) * sin * inv
            out = local_attention(q, k, v)
            out = out.transpose(0, 2, 1, 3).reshape(b, n, INNER)
            return out @ Wo

        def ffn_layer(x, g, bln, W1, b1, W2, b2):
            mu = x.mean(-1, keepdims=True)
            var = ((x - mu) ** 2).mean(-1, keepdims=True)
            xn = (x - mu) / jnp.sqrt(var + 1e-05) * g + bln
            hg = xn @ W1 + b1
            a, gate = jnp.split(hg, 2, -1)
            return a * jax.nn.gelu(gate, approximate=False) @ W2 + b2
        key = jax.random.key(seed)
        ks = jax.random.split(key, 8)
        B, N = (2, 256)
        init = lambda k, shape: jax.random.normal(k, shape, jnp.float32) * 0.02
        return {'x': jax.random.normal(ks[0], (B, N, DIM), jnp.float32), 'Wqkv': init(ks[1], (DEPTH, DIM, 3 * INNER)), 'q_scale': jnp.ones((DEPTH, DIM_HEAD), jnp.float32), 'k_scale': jnp.ones((DEPTH, DIM_HEAD), jnp.float32), 'Wo': init(ks[2], (DEPTH, INNER, DIM)), 'ln_g': jnp.ones((DEPTH, DIM), jnp.float32), 'ln_b': jnp.zeros((DEPTH, DIM), jnp.float32), 'W1': init(ks[3], (DEPTH, DIM, 2 * DIM_INNER)), 'b1': jnp.zeros((DEPTH, 2 * DIM_INNER), jnp.float32), 'W2': init(ks[4], (DEPTH, DIM_INNER, DIM)), 'b2': jnp.zeros((DEPTH, DIM), jnp.float32)}
    _L0_ffn_all = _L0_ffn_setup()
    _L0_ffn_in = {k: v for k, v in _L0_ffn_all.items() if k in ('Wqkv', 'q_scale', 'k_scale', 'Wo', 'ln_g', 'ln_b', 'W1', 'b1', 'W2', 'b2')}
    del _L0_ffn_all
    return {'x': x, 'ctx_512': ctx_512, 'L0_attn_key': _L0_attn_in['key'], 'L0_attn_value': _L0_attn_in['value'], 'L0_attn_time_maa_x': _L0_attn_in['time_maa_x'], 'L0_attn_time_maa_w': _L0_attn_in['time_maa_w'], 'L0_attn_time_maa_k': _L0_attn_in['time_maa_k'], 'L0_attn_time_maa_v': _L0_attn_in['time_maa_v'], 'L0_attn_time_maa_r': _L0_attn_in['time_maa_r'], 'L0_attn_time_maa_w1': _L0_attn_in['time_maa_w1'], 'L0_attn_time_maa_w2': _L0_attn_in['time_maa_w2'], 'L0_attn_time_decay': _L0_attn_in['time_decay'], 'L0_attn_time_decay_w1': _L0_attn_in['time_decay_w1'], 'L0_attn_time_decay_w2': _L0_attn_in['time_decay_w2'], 'L0_attn_time_faaaa': _L0_attn_in['time_faaaa'], 'L0_attn_W_r': _L0_attn_in['W_r'], 'L0_attn_W_k': _L0_attn_in['W_k'], 'L0_attn_W_v': _L0_attn_in['W_v'], 'L0_attn_W_o': _L0_attn_in['W_o'], 'L0_attn_ln_w': _L0_attn_in['ln_w'], 'L0_attn_ln_b': _L0_attn_in['ln_b'], 'L0_xattn_Wk': _L0_xattn_in['Wk'], 'L0_xattn_bk': _L0_xattn_in['bk'], 'L0_xattn_Wq': _L0_xattn_in['Wq'], 'L0_xattn_bq': _L0_xattn_in['bq'], 'L0_xattn_Wv': _L0_xattn_in['Wv'], 'L0_xattn_bv': _L0_xattn_in['bv'], 'L0_xattn_Wck': _L0_xattn_in['Wck'], 'L0_xattn_bck': _L0_xattn_in['bck'], 'L0_xattn_Wcq': _L0_xattn_in['Wcq'], 'L0_xattn_bcq': _L0_xattn_in['bcq'], 'L0_xattn_Wcv': _L0_xattn_in['Wcv'], 'L0_xattn_bcv': _L0_xattn_in['bcv'], 'L0_xattn_Wp': _L0_xattn_in['Wp'], 'L0_xattn_bp': _L0_xattn_in['bp'], 'L0_ffn_Wqkv': _L0_ffn_in['Wqkv'], 'L0_ffn_q_scale': _L0_ffn_in['q_scale'], 'L0_ffn_k_scale': _L0_ffn_in['k_scale'], 'L0_ffn_Wo': _L0_ffn_in['Wo'], 'L0_ffn_ln_g': _L0_ffn_in['ln_g'], 'L0_ffn_ln_b': _L0_ffn_in['ln_b'], 'L0_ffn_W1': _L0_ffn_in['W1'], 'L0_ffn_b1': _L0_ffn_in['b1'], 'L0_ffn_W2': _L0_ffn_in['W2'], 'L0_ffn_b2': _L0_ffn_in['b2']}

def reference(x, ctx_512, L0_attn_key, L0_attn_value, L0_attn_time_maa_x, L0_attn_time_maa_w, L0_attn_time_maa_k, L0_attn_time_maa_v, L0_attn_time_maa_r, L0_attn_time_maa_w1, L0_attn_time_maa_w2, L0_attn_time_decay, L0_attn_time_decay_w1, L0_attn_time_decay_w2, L0_attn_time_faaaa, L0_attn_W_r, L0_attn_W_k, L0_attn_W_v, L0_attn_W_o, L0_attn_ln_w, L0_attn_ln_b, L0_xattn_Wk, L0_xattn_bk, L0_xattn_Wq, L0_xattn_bq, L0_xattn_Wv, L0_xattn_bv, L0_xattn_Wck, L0_xattn_bck, L0_xattn_Wcq, L0_xattn_bcq, L0_xattn_Wcv, L0_xattn_bcv, L0_xattn_Wp, L0_xattn_bp, L0_ffn_Wqkv, L0_ffn_q_scale, L0_ffn_k_scale, L0_ffn_Wo, L0_ffn_ln_g, L0_ffn_ln_b, L0_ffn_W1, L0_ffn_b1, L0_ffn_W2, L0_ffn_b2):
    import jax
    import jax.numpy as jnp

    def _L0_attn_ref(query, key, value, time_maa_x, time_maa_w, time_maa_k, time_maa_v, time_maa_r, time_maa_w1, time_maa_w2, time_decay, time_decay_w1, time_decay_w2, time_faaaa, W_r, W_k, W_v, W_o, ln_w, ln_b):
        import jax, jax.numpy as jnp
        import numpy as np
        B, T, C = (4, 128, 128)
        HEAD = 64
        H = C // HEAD
        LORA_MIX = 32
        LORA_DECAY = 64
        LN_EPS = 0.00064

        def _wkv6(r, k, v, w, u):
            rT = jnp.moveaxis(r, 1, 0)
            kT = jnp.moveaxis(k, 1, 0)
            vT = jnp.moveaxis(v, 1, 0)
            wT = jnp.moveaxis(w, 1, 0)

            def step(S, inputs):
                rt, kt, vt, wt = inputs
                kv = kt[..., :, None] * vt[..., None, :]
                y = jnp.einsum('bhi,bhij->bhj', rt, S + u[None, :, :, None] * kv)
                S = wt[..., :, None] * S + kv
                return (S, y)
            S0 = jnp.zeros((r.shape[0], H, HEAD, HEAD), r.dtype)
            _, yT = jax.lax.scan(step, S0, (rT, kT, vT, wT))
            return jnp.moveaxis(yT, 0, 1)

        def _tmix_forward(x, time_maa_x, time_maa_w, time_maa_k, time_maa_v, time_maa_r, time_maa_w1, time_maa_w2, time_decay, time_decay_w1, time_decay_w2, time_faaaa, W_r, W_k, W_v, W_o, ln_w, ln_b):
            b, t, c = x.shape
            xshift = jnp.pad(x, ((0, 0), (1, 0), (0, 0)))[:, :t]
            xx = xshift - x
            xxx = x + xx * time_maa_x
            m = jnp.tanh(xxx @ time_maa_w1).reshape(b, t, 4, LORA_MIX)
            m = jnp.einsum('btfl,flc->fbtc', m, time_maa_w2)
            mw, mk, mv, mr = (m[0], m[1], m[2], m[3])
            xw = x + xx * (time_maa_w + mw)
            xk = x + xx * (time_maa_k + mk)
            xv = x + xx * (time_maa_v + mv)
            xr = x + xx * (time_maa_r + mr)
            r = (xr @ W_r).reshape(b, t, H, HEAD)
            k = (xk @ W_k).reshape(b, t, H, HEAD)
            v = (xv @ W_v).reshape(b, t, H, HEAD)
            ww = time_decay + jnp.tanh(xw @ time_decay_w1) @ time_decay_w2
            w = jnp.exp(-jnp.exp(ww)).reshape(b, t, H, HEAD)
            y = _wkv6(r, k, v, w, time_faaaa)
            mean = y.mean(-1, keepdims=True)
            var = y.var(-1, keepdims=True)
            yn = ((y - mean) * jax.lax.rsqrt(var + LN_EPS)).reshape(b, t, c)
            yn = yn * ln_w + ln_b
            return yn @ W_o
        return _tmix_forward(query, time_maa_x, time_maa_w, time_maa_k, time_maa_v, time_maa_r, time_maa_w1, time_maa_w2, time_decay, time_decay_w1, time_decay_w2, time_faaaa, W_r, W_k, W_v, W_o, ln_w, ln_b)

    def _L0_xattn_ref(x, cross_input, Wk, bk, Wq, bq, Wv, bv, Wck, bck, Wcq, bcq, Wcv, bcv, Wp, bp):
        import jax, jax.numpy as jnp
        import numpy as np
        B, T, TC, C, CC, H = (2, 256, 64, 128, 64, 16)
        D = C // H

        def _heads(t):
            b, l, _ = t.shape
            return t.reshape(b, l, H, D).transpose(0, 2, 1, 3)
        scale = np.float32(1.0 / np.sqrt(D))
        q = _heads(x @ Wq + bq)
        k = _heads(x @ Wk + bk)
        v = _heads(x @ Wv + bv)
        att = jnp.einsum('bhqd,bhkd->bhqk', q, k) * scale
        causal = jnp.tril(jnp.ones((T, T), bool))
        att = jnp.where(causal[None, None], att, -jnp.inf)
        y = jnp.einsum('bhqk,bhkd->bhqd', jax.nn.softmax(att, axis=-1), v)
        qc = _heads(x @ Wcq + bcq)
        kc = _heads(cross_input @ Wck + bck)
        vc = _heads(cross_input @ Wcv + bcv)
        attc = jnp.einsum('bhqd,bhkd->bhqk', qc, kc) * scale
        y = y + jnp.einsum('bhqk,bhkd->bhqd', jax.nn.softmax(attc, axis=-1), vc)
        y = y.transpose(0, 2, 1, 3).reshape(x.shape[0], T, C)
        return y @ Wp + bp

    def _L0_ffn_ref(x, Wqkv, q_scale, k_scale, Wo, ln_g, ln_b, W1, b1, W2, b2):
        import jax, jax.numpy as jnp
        import numpy as np
        DIM = 128
        DEPTH = 6
        HEADS = 16
        DIM_HEAD = 64
        WINDOW = 32
        INNER = HEADS * DIM_HEAD
        DIM_INNER = int(DIM * 4 * 2 / 3)
        QK_SCALE = 8.0

        def shift_tokens(t):
            a, s = jnp.split(t, 2, -1)
            s = jnp.pad(s, ((0, 0), (1, 0), (0, 0)))[:, :-1]
            return jnp.concatenate([a, s], -1)

        def l2norm(t):
            return t / jnp.maximum(jnp.linalg.norm(t, axis=-1, keepdims=True), 1e-12)

        def rotate_half(x):
            x1, x2 = jnp.split(x, 2, -1)
            return jnp.concatenate([-x2, x1], -1)

        def rotary_tables(n):
            half = jnp.arange(0, DIM_HEAD, 2, dtype=jnp.float32)
            inv_freq = 1.0 / 10000.0 ** (half / DIM_HEAD)
            t = jnp.arange(n, dtype=jnp.float32)
            freqs = t[:, None] * inv_freq[None, :]
            freqs = jnp.concatenate([freqs, freqs], -1)
            base_scale = (half + 0.4 * DIM_HEAD) / (1.4 * DIM_HEAD)
            power = (t - n // 2) / (WINDOW // 2)
            scale = base_scale[None, :] ** power[:, None]
            scale = jnp.concatenate([scale, scale], -1)
            return (freqs, scale)

        def local_attention(q, k, v):
            b, h, n, d = q.shape
            w = WINDOW
            nw = n // w
            bq = q.reshape(b, h, nw, w, d)
            bk = k.reshape(b, h, nw, w, d)
            bv = v.reshape(b, h, nw, w, d)

            def look(t):
                p = jnp.pad(t, ((0, 0), (0, 0), (1, 0), (0, 0), (0, 0)))
                return jnp.concatenate([p[:, :, :nw], p[:, :, 1:]], axis=3)
            bk2, bv2 = (look(bk), look(bv))
            seq = jnp.arange(n).reshape(nw, w)
            seq_p = jnp.pad(seq, ((1, 0), (0, 0)), constant_values=-1)
            jt = jnp.concatenate([seq_p[:nw], seq_p[1:]], axis=1)
            it = seq[:, :, None]
            jb = jt[:, None, :]
            mask = (it < jb) | (it > jb + w) | (jb == -1)
            sim = jnp.einsum('bhwie,bhwje->bhwij', bq, bk2) * QK_SCALE
            sim = jnp.where(mask, -jnp.finfo(sim.dtype).max, sim)
            attn = jax.nn.softmax(sim, -1)
            out = jnp.einsum('bhwij,bhwje->bhwie', attn, bv2)
            return out.reshape(b, h, n, d)

        def attn_layer(x, Wqkv, qs, ksc, Wo):
            b, n, _ = x.shape
            qkv = x @ Wqkv
            q, k, v = jnp.split(qkv, 3, -1)
            sh = lambda t: t.reshape(b, n, HEADS, DIM_HEAD).transpose(0, 2, 1, 3)
            q, k, v = (sh(q), sh(k), sh(v))
            q = l2norm(q) * qs
            k = l2norm(k) * ksc
            freqs, scale = rotary_tables(n)
            cos, sin = (jnp.cos(freqs), jnp.sin(freqs))
            q = q * cos * scale + rotate_half(q) * sin * scale
            inv = 1.0 / scale
            k = k * cos * inv + rotate_half(k) * sin * inv
            out = local_attention(q, k, v)
            out = out.transpose(0, 2, 1, 3).reshape(b, n, INNER)
            return out @ Wo

        def ffn_layer(x, g, bln, W1, b1, W2, b2):
            mu = x.mean(-1, keepdims=True)
            var = ((x - mu) ** 2).mean(-1, keepdims=True)
            xn = (x - mu) / jnp.sqrt(var + 1e-05) * g + bln
            hg = xn @ W1 + b1
            a, gate = jnp.split(hg, 2, -1)
            return a * jax.nn.gelu(gate, approximate=False) @ W2 + b2
        for i in range(DEPTH):
            x = attn_layer(shift_tokens(x), Wqkv[i], q_scale[i], k_scale[i], Wo[i]) + x
            x = ffn_layer(shift_tokens(x), ln_g[i], ln_b[i], W1[i], b1[i], W2[i], b2[i]) + x
        return x
    x = _layernorm(x + _L0_attn_ref(x, L0_attn_key, L0_attn_value, L0_attn_time_maa_x, L0_attn_time_maa_w, L0_attn_time_maa_k, L0_attn_time_maa_v, L0_attn_time_maa_r, L0_attn_time_maa_w1, L0_attn_time_maa_w2, L0_attn_time_decay, L0_attn_time_decay_w1, L0_attn_time_decay_w2, L0_attn_time_faaaa, L0_attn_W_r, L0_attn_W_k, L0_attn_W_v, L0_attn_W_o, L0_attn_ln_w, L0_attn_ln_b), axis=-1)
    x = _layernorm(x + _L0_xattn_ref(x, ctx_512, L0_xattn_Wk, L0_xattn_bk, L0_xattn_Wq, L0_xattn_bq, L0_xattn_Wv, L0_xattn_bv, L0_xattn_Wck, L0_xattn_bck, L0_xattn_Wcq, L0_xattn_bcq, L0_xattn_Wcv, L0_xattn_bcv, L0_xattn_Wp, L0_xattn_bp), axis=-1)
    x = _layernorm(x + _L0_ffn_ref(x, L0_ffn_Wqkv, L0_ffn_q_scale, L0_ffn_k_scale, L0_ffn_Wo, L0_ffn_ln_g, L0_ffn_ln_b, L0_ffn_W1, L0_ffn_b1, L0_ffn_W2, L0_ffn_b2), axis=-1)
    return x

_drawn_inputs = setup_inputs


def setup_inputs(seed=0):
    import zlib

    import numpy as np

    out = dict(_drawn_inputs(seed))
    spreads = {'L0_attn_ln_w': (1.0, 0.2),
     'L0_attn_ln_b': (0.0, 0.1),
     'L0_xattn_bk': (0.0, 0.8),
     'L0_xattn_bq': (0.0, 0.458),
     'L0_xattn_bv': (0.0, 0.1),
     'L0_xattn_bck': (0.0, 0.8),
     'L0_xattn_bcq': (0.0, 0.389),
     'L0_xattn_bcv': (0.0, 0.1),
     'L0_xattn_bp': (0.0, 0.1),
     'L0_ffn_q_scale': (1.0, 0.6),
     'L0_ffn_k_scale': (1.0, 0.6),
     'L0_ffn_ln_g': (1.0, 0.6),
     'L0_ffn_ln_b': (0.0, 0.8),
     'L0_ffn_b1': (0.0, 0.8),
     'L0_ffn_b2': (0.0, 0.1)}
    factors = {'L0_attn_time_maa_x': 8.0,
     'L0_attn_time_maa_w': 8.0,
     'L0_attn_time_maa_w1': 5.542,
     'L0_attn_time_maa_w2': 5.554,
     'L0_attn_time_decay_w1': 8.0,
     'L0_attn_time_decay_w2': 8.0,
     'L0_attn_time_faaaa': 2.927,
     'L0_ffn_W1': 3.691,
     'L0_ffn_W2': 3.612}
    for name, (base, spread) in spreads.items():
        noise = np.random.default_rng([zlib.crc32(name.encode()), seed]).standard_normal(out[name].shape)
        drawn = base * np.exp(spread * noise) if base else spread * noise
        out[name] = jnp.asarray(drawn.astype(out[name].dtype))
    for name, factor in factors.items():
        out[name] = (out[name] * factor).astype(out[name].dtype)
    return out
```

```python
from contextlib import ExitStack

import concourse.bass as bass
from concourse import mybir

F32 = mybir.dt.float32
BF16 = mybir.dt.bfloat16
I32 = mybir.dt.int32
ALU = mybir.AluOpType
ACT = mybir.ActivationFunctionType
AX_X = mybir.AxisListType.X

P = 128
B, T = 4, 256
N = B * T
TILES = T // P
HALF = 512

RH, RD = 2, 64
LEVELS = 8
GN_EPS, LN_EPS = 0.00064, 1e-05
XH, XD, CTX, CC = 16, 8, 64, 64
XPAD = 32
HG = 4
DEPTH, LH, LD, WIN = 6, 16, 64, 32
PAIRS = LH // 2
SEG = WIN + P
INNER = 341
FC = [(0, 128), (128, 128), (256, 85)]
QK_SCALE = 8.0
BIG = 1.0e30
LN_EXP = "natural_log_exp_and_others"
SS_SCALE = float(2 ** 20)


def build(nc, t):
    with ExitStack() as ctx:
        def sb(name, shape, dt=F32):
            return ctx.enter_context(nc.sbuf_tensor(name, shape, dt))

        def sem(name):
            return ctx.enter_context(nc.semaphore(name))

        psum = ctx.enter_context(nc.psum_tensor("psum", [P, 8 * HALF], F32))
        ps = [psum[:, i * HALF:(i + 1) * HALF] for i in range(8)]
        g = {
            "sb": sb, "sem": sem, "ps": ps, "psum": psum, "t": t, "ctx": ctx,
            "ident": sb("identity", [P, P]), "identb": sb("identity_bf16", [P, P], BF16),
            "ones": sb("channel_mean", [P, P]), "blk": sb("head_mean", [P, P]), "eps": sb("epsilons", [P, 4]),
            "X": sb("X", [P, N]), "Z": sb("Z", [P, N]),
        }
        with ExitStack() as scope:
            time_mix(nc, g, scope)
        layer_norm(nc, g, "ln1", g["Z"], g["X"])
        with ExitStack() as scope:
            cross_attention(nc, g, scope)
        layer_norm(nc, g, "ln2", g["Z"], g["X"])
        with ExitStack() as scope:
            local_layers(nc, g, scope)
        layer_norm(nc, g, "ln3", g["Z"], g["X"], out=t["out"])


def layer_norm(nc, g, name, src, dst, out=None):
    ps = g["ps"]
    with ExitStack() as scope:
        xc = scope.enter_context(nc.sbuf_tensor(f"{name}_xc", [P, N], F32))
        sq = scope.enter_context(nc.sbuf_tensor(f"{name}_sq", [P, N], F32))
        names = ["mean", "centred", "squared", "var", "logvar", "rstd", "normed", "stored"]
        s = {n: g["sem"](f"{name}_{n}") for n in names}
        block = scope.enter_context(nc.Block())
        col = [slice(c * HALF, (c + 1) * HALF) for c in range(2)]

        @block.tensor
        def _(pe):
            for c in range(2):
                nc.tensor.matmul(ps[c][:, :], g["ones"][:, :], src[:, col[c]], start=True, stop=True).then_inc(s["mean"], 1)
            for c in range(2):
                pe.wait_ge(s["squared"], c + 1)
                nc.tensor.matmul(ps[2 + c][:, :], g["ones"][:, :], sq[:, col[c]], start=True, stop=True).then_inc(s["var"], 1)

        @block.vector
        def _(dve):
            for c in range(2):
                dve.wait_ge(s["mean"], c + 1)
                nc.vector.tensor_tensor(xc[:, col[c]], src[:, col[c]], ps[c][:, :], ALU.subtract).then_inc(s["centred"], 1)
            for c in range(2):
                dve.wait_ge(s["centred"], c + 1)
                dve.wait_ge(s["rstd"], c + 1)
                nc.vector.tensor_tensor(dst[:, col[c]], xc[:, col[c]], sq[:, col[c]], ALU.mult).then_inc(s["normed"], 1)

        @block.scalar
        def _(act):
            for c in range(2):
                act.wait_ge(s["centred"], c + 1)
                nc.scalar.activation(sq[:, col[c]], xc[:, col[c]], ACT.Square).then_inc(s["squared"], 1)
            for c in range(2):
                act.wait_ge(s["var"], c + 1)
                nc.scalar.activation(sq[:, col[c]], ps[2 + c][:, :], ACT.Ln, bias=g["eps"][:, 0:1]).then_inc(s["logvar"], 1)
            for c in range(2):
                act.wait_ge(s["logvar"], c + 1)
                nc.scalar.activation(sq[:, col[c]], sq[:, col[c]], ACT.Exp, scale=-0.5).then_inc(s["rstd"], 1)

        @block.sync
        def _(sp):
            if out is not None:
                for c in range(2):
                    sp.wait_ge(s["normed"], c + 1)
                    sp.dma_start(out[:, col[c]], dst[:, col[c]]).then_inc(s["stored"], 16)
                sp.wait_ge(s["stored"], 32)


def time_mix(nc, g, scope):
    ps, t, sem = g["ps"], g["t"], g["sem"]

    def sb(name, shape, dt=F32):
        return scope.enter_context(nc.sbuf_tensor(f"tm_{name}", shape, dt))

    x = sb("x", [P, N])
    vec = sb("vec", [P, 9])
    wts = sb("wts", [P, 6 * P + 64])
    dw2 = sb("dw2", [64, P])
    masks = sb("masks", [P, LEVELS, P], I32)
    xx = sb("xx", [P, N])
    mixed = sb("mixed", [P, 4, N])
    m = sb("m", [P, N])
    R2 = sb("R2", [P, RH, N])
    K = sb("K", [P, N])
    V = sb("V", [P, N])
    w = sb("w", [P, N])
    bp = [w, sb("bp1", [P, N // 2]), sb("bp2", [P, N // 4])]
    pre = sb("pre", [P, N])
    suf = sb("suf", [P, N])
    rp = [sb(f"rp{i}", [P, RH, N]) for i in range(2)]
    kp = [sb(f"kp{i}", [P, N]) for i in range(2)]
    S = sb("S", [P, 4 * HALF])
    SX = sb("SX", [P, 2 * HALF])
    Y = sb("Y", [P, N])
    yc = sb("yc", [P, N])
    sq = sb("sq", [P, N])
    W = {n: wts[:, i * P:(i + 1) * P] for i, n in enumerate(["w1", "w2", "r", "k", "v", "o"])}
    dw1 = wts[:, 6 * P:6 * P + 64]
    col = [slice(c * HALF, (c + 1) * HALF) for c in range(2)]
    bt = lambda a: a[:, :].rearrange("p (b t) -> p b t", b=B)

    names = ["in", "consts", "prep", "xx", "xxx", "m1", "mt", "m2", "mulx", "addx", "rps", "kps", "vps", "lps", "rev", "kev",
             "vev", "lev", "dps", "dev", "wev", "ku", "bpr", "pre", "suf", "kpr", "rpr", "gps", "gcp", "xev", "yps", "yev",
             "mean", "centred", "squared", "var", "logvar", "rstd", "yn", "yna", "ops"]
    s = {n: sem(f"tm_{n}") for n in names}
    block = scope.enter_context(nc.Block())

    @block.sync
    def _(sp):
        sp.dma_start(x[:, :], t["xT"]).then_inc(s["in"], 16)
        sp.dma_start(vec[:, :], t["tm_vec"]).then_inc(s["in"], 16)
        sp.dma_start(wts[:, :], t["tm_w"]).then_inc(s["in"], 16)
        sp.dma_start(dw2[:, :], t["tm_dw2"]).then_inc(s["in"], 16)
        sp.dma_start(masks[:, :, :], t["tm_masks"]).then_inc(s["consts"], 16)
        sp.dma_start(g["ident"][:, :], t["ident"]).then_inc(s["consts"], 16)
        sp.dma_start(g["identb"][:, :], t["identb"]).then_inc(s["consts"], 16)
        sp.dma_start(g["ones"][:, :], t["ones"]).then_inc(s["consts"], 16)
        sp.dma_start(g["blk"][:, :], t["blk"]).then_inc(s["consts"], 16)
        sp.dma_start(g["eps"][:, :], t["eps"]).then_inc(s["consts"], 16)

    NCONST = 6 * 16

    @block.gpsimd
    def _(pool):
        for f in range(4):
            pool.wait_ge(s["mulx"], 2 * (f + 1))
            nc.gpsimd.tensor_tensor(mixed[:, f, :], mixed[:, f, :], x[:, :], ALU.add).then_inc(s["addx"], 1)
        pool.wait_ge(s["kev"], 2)
        for lv in range(1, LEVELS):
            pool.wait_ge(s["suf"], lv)
            if lv >= 2:
                pool.wait_ge(s["gps"], lv)
            nc.gpsimd.tensor_tensor(kp[lv % 2][:, :], K[:, :], suf[:, :], ALU.mult).then_inc(s["kpr"], 1)

    @block.vector
    def _(dve):
        nc.vector.memset(R2[:, :, :], 0.0).then_inc(s["prep"], 1)
        nc.vector.memset(S[:, :], 0.0).then_inc(s["prep"], 1)
        nc.vector.memset(pre[:, :], 1.0).then_inc(s["prep"], 1)
        nc.vector.memset(suf[:, :], 1.0).then_inc(s["prep"], 1)
        dve.wait_ge(s["in"], 64)
        nc.vector.tensor_tensor(bt(xx)[:, :, 1:], bt(x)[:, :, :T - 1], bt(x)[:, :, 1:], ALU.subtract).then_inc(s["xx"], 1)
        nc.vector.tensor_scalar(bt(xx)[:, :, 0:1], bt(x)[:, :, 0:1], -1.0, None, ALU.mult).then_inc(s["xx"], 1)
        dve.wait_ge(s["xx"], 2)
        nc.vector.scalar_tensor_tensor(yc[:, :], xx[:, :], vec[:, 0:1], x[:, :], ALU.mult, ALU.add).then_inc(s["xxx"], 1)
        for f in range(4):
            for c in range(2):
                dve.wait_ge(s["m2"], 2 * f + c + 1)
                nc.vector.scalar_tensor_tensor(mixed[:, f, col[c]], ps[2 * f + c][:, :], vec[:, 1 + f:2 + f], xx[:, col[c]],
                                               ALU.add, ALU.mult).then_inc(s["mulx"], 1)
        dve.wait_ge(s["kev"], 2)
        nc.vector.tensor_scalar(kp[0][:, :], K[:, :], vec[:, 6:7], None, ALU.mult).then_inc(s["ku"], 1)
        dve.wait_ge(s["consts"], NCONST)

        def select(step, mask):
            dve.wait_ge(s["gps"], step + 1)
            if step:
                dve.wait_ge(s["gcp"], step)
            for h in range(4):
                i = nc.vector.copy_predicated(S[:, h * HALF:(h + 1) * HALF].rearrange("p (n t) -> p n t", t=P),
                                              masks[:, mask:mask + 1, :].broadcast_to([P, 4, P]),
                                              ps[4 * (step % 2) + h][:, :].rearrange("p (n t) -> p n t", t=P))
            i.then_inc(s["gcp"], 1)

        dve.wait_ge(s["wev"], 2)
        dve.wait_ge(s["prep"], 4)
        dve.wait_ge(s["rev"], 4)
        for lv in range(1, LEVELS):
            mm = 1 << (lv - 1)
            halves = lambda a: a[:, :].rearrange("p (n h m) -> p n h m", h=2, m=mm)
            whole = bp[0] if lv == 1 else bp[1 + (lv - 2) % 2]
            n = N // (2 * mm)
            wv = whole[:, :2 * n].rearrange("p (n h) -> p n h", h=2)
            if lv >= 2:
                dve.wait_ge(s["bpr"], lv - 1)
                dve.wait_ge(s["kpr"], lv - 1)
                dve.wait_ge(s["rpr"], lv - 1)
                dve.wait_ge(s["suf"], lv - 1)
            nc.vector.tensor_tensor(halves(suf)[:, :, 0, :], halves(suf)[:, :, 0, :],
                                    wv[:, :, 1:2].broadcast_to([P, n, mm]), ALU.mult).then_inc(s["suf"], 1)
            nc.vector.tensor_tensor(halves(pre)[:, :, 1, :], halves(pre)[:, :, 1, :],
                                    wv[:, :, 0:1].broadcast_to([P, n, mm]), ALU.mult).then_inc(s["pre"], 1)
            nxt = bp[1 + (lv - 1) % 2]
            nc.vector.tensor_tensor(nxt[:, :n].rearrange("p (n o) -> p n o", o=1), wv[:, :, 0:1], wv[:, :, 1:2],
                                    ALU.mult).then_inc(s["bpr"], 1)
            dve.wait_ge(s["pre"], lv)
            if lv >= 3:
                dve.wait_ge(s["gps"], lv)
            nc.vector.tensor_tensor(rp[lv % 2][:, :, :], R2[:, :, :],
                                    pre[:, :].rearrange("p (o n) -> p o n", o=1).broadcast_to([P, RH, N]),
                                    ALU.mult).then_inc(s["rpr"], 1)
            select(lv - 1, lv - 1)
        select(LEVELS - 1, LEVELS - 1)
        for c in range(2):
            dve.wait_ge(s["yev"], c + 1)
            dve.wait_ge(s["mean"], c + 1)
            nc.vector.tensor_tensor(yc[:, col[c]], Y[:, col[c]], ps[c][:, :], ALU.subtract).then_inc(s["centred"], 1)
        for c in range(2):
            dve.wait_ge(s["centred"], c + 1)
            dve.wait_ge(s["rstd"], c + 1)
            nc.vector.tensor_tensor(yc[:, col[c]], yc[:, col[c]], sq[:, col[c]], ALU.mult).then_inc(s["yn"], 1)
            dve.wait_ge(s["yn"], c + 1)
            nc.vector.tensor_scalar(yc[:, col[c]], yc[:, col[c]], vec[:, 7:8], vec[:, 8:9], ALU.mult, ALU.add).then_inc(s["yna"], 1)
        for c in range(2):
            dve.wait_ge(s["ops"], c + 1)
            nc.vector.tensor_tensor(g["Z"][:, col[c]], x[:, col[c]], ps[4 + c][:, :], ALU.add)

    @block.scalar
    def _(act):
        for c in range(2):
            act.wait_ge(s["m1"], c + 1)
            nc.scalar.activation(m[:, col[c]], ps[c][:, :], ACT.Tanh).then_inc(s["mt"], 1)
        for c in range(2):
            act.wait_ge(s["lps"], c + 1)
            nc.scalar.activation(m[0:64, col[c]], ps[c][0:64, :], ACT.Tanh).then_inc(s["lev"], 1)
        for c in range(2):
            act.wait_ge(s["kps"], c + 1)
            nc.scalar.copy(K[:, col[c]], ps[2 + c][:, :]).then_inc(s["kev"], 1)
        for c in range(2):
            act.wait_ge(s["dps"], c + 1)
            nc.scalar.activation(w[:, col[c]], ps[c][:, :], ACT.Exp, bias=vec[:, 5:6]).then_inc(s["dev"], 1)
            act.wait_ge(s["dev"], c + 1)
            nc.scalar.activation(w[:, col[c]], w[:, col[c]], ACT.Exp, scale=-1.0).then_inc(s["wev"], 1)
        for c in range(2):
            act.wait_ge(s["vps"], c + 1)
            nc.scalar.copy(V[:, col[c]], ps[4 + c][:, :]).then_inc(s["vev"], 1)
        act.wait_ge(s["prep"], 1)
        for c in range(2):
            act.wait_ge(s["rps"], c + 1)
            for h in range(RH):
                r = slice(h * RD, (h + 1) * RD)
                nc.scalar.copy(R2[r, h, col[c]], ps[6 + c][r, :]).then_inc(s["rev"], 1)
        nc.scalar.preload_act_table_set(LN_EXP)
        act.wait_ge(s["gps"], LEVELS + 1)
        for c in range(2):
            nc.scalar.copy(SX[:, col[c]], ps[c][:, :]).then_inc(s["xev"], 1)
        for c in range(2):
            act.wait_ge(s["yps"], c + 1)
            nc.scalar.copy(Y[:, col[c]], ps[4 + c][:, :]).then_inc(s["yev"], 1)
        for c in range(2):
            act.wait_ge(s["centred"], c + 1)
            nc.scalar.activation(sq[:, col[c]], yc[:, col[c]], ACT.Square).then_inc(s["squared"], 1)
        for c in range(2):
            act.wait_ge(s["var"], c + 1)
            nc.scalar.activation(sq[:, col[c]], ps[2 + c][:, :], ACT.Ln, bias=g["eps"][:, 1:2]).then_inc(s["logvar"], 1)
        for c in range(2):
            act.wait_ge(s["logvar"], c + 1)
            nc.scalar.activation(sq[:, col[c]], sq[:, col[c]], ACT.Exp, scale=-0.5).then_inc(s["rstd"], 1)

    @block.tensor
    def _(pe):
        pe.wait_ge(s["in"], 64)
        pe.wait_ge(s["xxx"], 1)
        for c in range(2):
            nc.tensor.matmul(ps[c][:, :], W["w1"], yc[:, col[c]], start=True, stop=True).then_inc(s["m1"], 1)
        for f in range(4):
            for c in range(2):
                pe.wait_ge(s["mt"], c + 1 if f else 2)
                q = slice(32 * f, 32 * f + 32)
                nc.tensor.matmul(ps[2 * f + c][:, :], W["w2"][q, :], m[q, col[c]], start=True, stop=True).then_inc(s["m2"], 1)
        pe.wait_ge(s["addx"], 1)
        for c in range(2):
            nc.tensor.matmul(ps[c][0:64, :], dw1, mixed[:, 0, col[c]], start=True, stop=True).then_inc(s["lps"], 1)
        pe.wait_ge(s["addx"], 2)
        for c in range(2):
            nc.tensor.matmul(ps[2 + c][:, :], W["k"], mixed[:, 1, col[c]], start=True, stop=True).then_inc(s["kps"], 1)
        for c in range(2):
            pe.wait_ge(s["lev"], c + 1)
            nc.tensor.matmul(ps[c][:, :], dw2[:, :], m[0:64, col[c]], start=True, stop=True).then_inc(s["dps"], 1)
        pe.wait_ge(s["addx"], 3)
        for c in range(2):
            for i in range(4):
                tok = slice((4 * c + i) * P, (4 * c + i + 1) * P)
                o = nc.tensor.matmul(ps[4 + c][:, i * P:(i + 1) * P], mixed[:, 2, tok], W["v"], start=True, stop=True)
            o.then_inc(s["vps"], 1)
        pe.wait_ge(s["addx"], 4)
        for c in range(2):
            nc.tensor.matmul(ps[6 + c][:, :], W["r"], mixed[:, 3, col[c]], start=True, stop=True).then_inc(s["rps"], 1)

        def scores(step, kk, rr):
            for bi in range(B * TILES):
                tok = slice(bi * P, (bi + 1) * P)
                o = nc.tensor.matmul(ps[4 * (step % 2) + bi // 2][:, (bi % 2) * 2 * P:(bi % 2 + 1) * 2 * P],
                                     kk[:, tok], rr[:, :, tok], start=True, stop=True)
            o.then_inc(s["gps"], 1)

        pe.wait_ge(s["ku"], 1)
        pe.wait_ge(s["rev"], 4)
        pe.wait_ge(s["wev"], 2)
        scores(0, kp[0], R2)
        pe.wait_ge(s["vev"], 2)
        pe.wait_ge(s["consts"], NCONST)
        scores(1, K, R2)
        for lv in range(1, LEVELS - 1):
            pe.wait_ge(s["kpr"], lv)
            pe.wait_ge(s["rpr"], lv)
            pe.wait_ge(s["gcp"], lv)
            scores(lv + 1, kp[lv % 2], rp[lv % 2])
        lv = LEVELS - 1
        pe.wait_ge(s["kpr"], lv)
        pe.wait_ge(s["rpr"], lv)
        pe.wait_ge(s["gcp"], lv)
        for b in range(B):
            o = nc.tensor.matmul(ps[b // 2][:, (b % 2) * 2 * P:(b % 2 + 1) * 2 * P],
                                 kp[lv % 2][:, b * T:b * T + P], rp[lv % 2][:, :, b * T + P:(b + 1) * T], start=True, stop=True)
        o.then_inc(s["gps"], 1)
        pe.wait_ge(s["xev"], 2)
        pe.wait_ge(s["gcp"], LEVELS)
        for c in range(2):
            for b in (2 * c, 2 * c + 1):
                for h in range(RH):
                    r = slice(h * RD, (h + 1) * RD)
                    o0 = (b % 2) * T
                    vt = lambda i: V[:, (b * TILES + i) * P + h * RD:(b * TILES + i) * P + (h + 1) * RD]
                    st = lambda i: S[:, ((b * TILES + i) * RH + h) * P:((b * TILES + i) * RH + h + 1) * P]
                    nc.tensor.matmul(ps[4 + c][r, o0:o0 + P], vt(0), st(0), start=True, stop=True)
                    nc.tensor.matmul(ps[4 + c][r, o0 + P:o0 + T], vt(0), SX[:, (b * RH + h) * P:(b * RH + h + 1) * P], start=True, stop=False)
                    o = nc.tensor.matmul(ps[4 + c][r, o0 + P:o0 + T], vt(1), st(1), start=False, stop=True)
            o.then_inc(s["yps"], 1)
        for c in range(2):
            pe.wait_ge(s["yev"], c + 1)
            nc.tensor.matmul(ps[c][:, :], g["blk"][:, :], Y[:, col[c]], start=True, stop=True).then_inc(s["mean"], 1)
        for c in range(2):
            pe.wait_ge(s["squared"], c + 1)
            nc.tensor.matmul(ps[2 + c][:, :], g["blk"][:, :], sq[:, col[c]], start=True, stop=True).then_inc(s["var"], 1)
        for c in range(2):
            pe.wait_ge(s["yna"], c + 1)
            nc.tensor.matmul(ps[4 + c][:, :], W["o"], yc[:, col[c]], start=True, stop=True).then_inc(s["ops"], 1)


def cross_attention(nc, g, scope):
    ps, t, sem, X, Z = g["ps"], g["t"], g["sem"], g["X"], g["Z"]
    ident, identb = g["ident"], g["identb"]
    GROUPS = XH // HG
    VW = XH * XPAD
    SCALE = XD ** -0.5

    def sb(name, shape, dt=F32):
        return scope.enter_context(nc.sbuf_tensor(f"xa_{name}", shape, dt))

    wts = sb("wts", [P, 3 * P + VW + GROUPS * P])
    cw = sb("cw", [CC, P + VW])
    vec = sb("vec", [P, 5])
    vb = sb("vb", [P, 2, VW])
    ctxT = sb("ctxT", [CC, B * P])
    hm = sb("hm", [P, XH])
    causal = sb("causal", [P, 2, 2 * T], BF16)
    xb = sb("xb", [P, T])
    cb = sb("cb", [CC, P])
    qT, kT, qcT, kcT = (sb(n, [P, T]) for n in ("qT", "kT", "qcT", "kcT"))
    kz = sb("kz", [P, XH, T])
    kcz = sb("kcz", [P, XH, CTX])
    V = sb("V", [P, TILES, VW])
    Vc = sb("Vc", [P, XH // 2, 2 * XPAD])
    Pb = [sb(f"Pb{i}", [P, 4 * HALF]) for i in range(2)]
    PT = [sb(f"PT{i}", [P, 2 * HALF]) for i in range(2)]
    mx, sm, rc = (sb(n, [P, 2, 16]) for n in ("mx", "sm", "rc"))
    Y = sb("Y", [P, GROUPS, T])
    Wq, Wk, Wcq = (wts[:, i * P:(i + 1) * P] for i in range(3))
    Wv = wts[:, 3 * P:3 * P + VW]
    Wp = wts[:, 3 * P + VW:].rearrange("p (g c) -> p g c", g=GROUPS)

    def parts(a):
        return [(a[:, 0:2 * HALF].rearrange("p (h k) -> p h k", k=T), 0, 4, T),
                (a[:, 2 * HALF:3 * HALF].rearrange("p (h k) -> p h k", k=P), 4, 8, P),
                (a[:, 3 * HALF:4 * HALF].rearrange("p (h k) -> p h k", k=CTX), 8, 16, CTX)]

    def psum_parts():
        r = lambda b, k: ps[b][:, :].rearrange("p (h k) -> p h k", k=k)
        return [(r(0, T), 0, 2, T), (r(1, T), 2, 4, T), (r(2, P), 4, 8, P), (r(3, CTX), 8, 16, CTX)]

    def sbuf_parts(a):
        r = lambda b, k: a[:, b * HALF:(b + 1) * HALF].rearrange("p (h k) -> p h k", k=k)
        return [r(0, T), r(1, T), r(2, P), r(3, CTX)]

    col = lambda a, i, lo, hi, n: a[:, i, lo:hi].rearrange("p (h o) -> p h o", o=1).broadcast_to([P, hi - lo, n])

    names = ["in", "zero", "xb", "qps", "kps", "qcps", "kcps", "vps", "vcps", "qev", "kev", "qcev", "kcev", "kz", "kcz", "vev", "vcev",
             "sps", "max", "sub", "exp", "sum", "rc", "pn", "tps", "pev", "yps", "yev", "wps", "res"]
    s = {n: sem(f"xa_{n}") for n in names}
    block = scope.enter_context(nc.Block())

    @block.sync
    def _(sp):
        for dst, src in ((wts[:, :], "xa_w"), (cw[:, :], "xa_cw"), (vec[:, :], "xa_vec"), (vb[:, :, :], "xa_vb"),
                         (ctxT[:, :], "ctxT"), (hm[:, :], "xa_hm"), (causal[:, :, :], "xa_causal")):
            sp.dma_start(dst, t[src]).then_inc(s["in"], 16)

    NIN = 7 * 16

    @block.tensor
    def _(pe):
        pe.wait_ge(s["in"], NIN)

        def scores(b, u):
            hs = slice(HG * u, HG * u + HG)
            if u:
                pe.wait_ge(s["sub"], GROUPS * b + u)
            for i in range(2):
                nc.tensor.matmul(ps[i][:, :], identb[:, :], causal[:, 1, :], start=True, stop=False)
                nc.tensor.matmul(ps[i][:, :], qT[:, P:T], kz[:, HG * u + 2 * i:HG * u + 2 * i + 2, :], start=False, stop=True)
            nc.tensor.matmul(ps[2][:, :], identb[:, :], causal[:, 0, :], start=True, stop=False)
            nc.tensor.matmul(ps[2][:, :], qT[:, 0:P], kz[:, hs, 0:P], start=False, stop=True)
            for i in range(TILES):
                o = nc.tensor.matmul(ps[3][:, i * T:(i + 1) * T], qcT[:, i * P:(i + 1) * P], kcz[:, hs, :], start=True, stop=True)
            o.then_inc(s["sps"], 1)

        with pe.Fori(0, B) as b:
            pe.wait_ge(s["xb"], 2 * b + 2)
            nc.tensor.matmul(ps[1][:, 0:T], Wk, xb[:, :], start=True, stop=True).then_inc(s["kps"], 1)
            nc.tensor.matmul(ps[0][:, 0:T], Wq, xb[:, :], start=True, stop=True).then_inc(s["qps"], 1)
            nc.tensor.matmul(ps[3][:, 0:CTX], cw[:, 0:P], cb[:, 0:CTX], start=True, stop=True).then_inc(s["kcps"], 1)
            nc.tensor.matmul(ps[2][:, 0:T], Wcq, xb[:, :], start=True, stop=True).then_inc(s["qcps"], 1)
            for i in range(TILES):
                nc.tensor.matmul(ps[4 + i][:, :], xb[:, i * P:(i + 1) * P], Wv, start=True, stop=True).then_inc(s["vps"], 1)
            nc.tensor.matmul(ps[6][:, :], cb[:, :], cw[:, P:], start=True, stop=True).then_inc(s["vcps"], 1)
            pe.wait_ge(s["kz"], 16 * b + 16)
            pe.wait_ge(s["kcz"], b + 1)
            pe.wait_ge(s["qev"], b + 1)
            pe.wait_ge(s["qcev"], b + 1)
            scores(b, 0)
            for u in range(GROUPS):
                if u + 1 < GROUPS:
                    scores(b, u + 1)
                p = Pb[u % 2]
                pe.wait_ge(s["pn"], 3 * GROUPS * b + 3 * (u + 1))
                for i in range(2):
                    if u or i:
                        pe.wait_ge(s["pev"], 2 * (2 * GROUPS * b + 2 * u + i))
                    else:
                        pe.wait_ge(s["vev"], 2 * b + 2)
                    for h in range(2):
                        hh = 2 * i + h
                        q1 = hh * T
                        q0 = 2 * HALF + hh * P
                        nc.tensor.transpose(ps[4][:, h * T:h * T + P], p[:, q0:q0 + P], ident[:, :])
                        nc.tensor.transpose(ps[4][:, h * T + P:(h + 1) * T], p[:, q1:q1 + P], ident[:, :])
                        nc.tensor.transpose(ps[5][:, h * P:(h + 1) * P], p[:, q1 + P:q1 + T], ident[:, :])
                    for q in range(TILES):
                        c0 = 3 * HALF + q * T + i * P
                        o = nc.tensor.transpose(ps[5][:, T + q * P:T + (q + 1) * P], p[:, c0:c0 + P], ident[:, :])
                    o.then_inc(s["tps"], 1)
                    pe.wait_ge(s["pev"], 2 * (2 * GROUPS * b + 2 * u + i + 1))
                    if i == 0:
                        if u:
                            pe.wait_ge(s["yev"], GROUPS * b + u)
                        else:
                            pe.wait_ge(s["vcev"], 2 * b + 2)
                    pt = PT[i]
                    for h in range(2):
                        hh = 2 * i + h
                        v = slice((HG * u + hh) * XPAD, (HG * u + hh + 1) * XPAD)
                        r = slice(XPAD * hh, XPAD * hh + XPAD)
                        nc.tensor.matmul(ps[6][r, 0:T], V[:, 0, v], pt[:, h * T:(h + 1) * T], start=True, stop=False, skip_group_check=True)
                        nc.tensor.matmul(ps[6][r, P:T], V[:, 1, v], pt[:, HALF + h * P:HALF + (h + 1) * P], start=False, stop=False, skip_group_check=True)
                    o = nc.tensor.matmul(ps[6][64 * i:64 * i + 64, 0:T], Vc[:, 2 * u + i, :], pt[:, HALF + T:], start=False, stop=True, skip_group_check=True)
                o.then_inc(s["yps"], 1)
            pe.wait_ge(s["yev"], GROUPS * b + GROUPS)
            for u in range(GROUPS):
                o = nc.tensor.matmul(ps[7][:, 0:T], Wp[:, u, :], Y[:, u, :], start=(u == 0), stop=(u == GROUPS - 1))
            o.then_inc(s["wps"], 1)

    @block.vector
    def _(dve):
        nc.vector.memset(Vc[:, :, :], 0.0).then_inc(s["zero"], 1)
        dve.wait_ge(s["in"], NIN)
        dve.wait_ge(s["zero"], 1)
        with dve.Fori(0, B) as b:
            nc.vector.tensor_copy(xb[:, :], X[:, bass.ds(b * T, T)]).then_inc(s["xb"], 1)
            nc.vector.tensor_copy(cb[:, :], ctxT[:, bass.ds(b * P, P)]).then_inc(s["xb"], 1)
            dve.wait_ge(s["kev"], b + 1)
            for h in range(XH):
                nc.vector.tensor_scalar(kz[:, h, :], kT[:, :], hm[:, h:h + 1], None, ALU.mult).then_inc(s["kz"], 1)
            dve.wait_ge(s["kcev"], b + 1)
            nc.vector.tensor_tensor(kcz[:, :, :], kcT[:, 0:CTX].rearrange("p (o k) -> p o k", o=1).broadcast_to([P, XH, CTX]),
                                    hm[:, :].rearrange("p (h o) -> p h o", o=1).broadcast_to([P, XH, CTX]), ALU.mult).then_inc(s["kcz"], 1)
            for i in range(TILES):
                dve.wait_ge(s["vps"], 2 * b + i + 1)
                nc.vector.tensor_tensor(V[:, i, :], ps[4 + i][:, :], vb[:, 0, :], ALU.add).then_inc(s["vev"], 1)
            dve.wait_ge(s["vcps"], b + 1)
            for h in range(2):
                r = slice(64 * h, 64 * h + 64)
                pair = lambda a: a.rearrange("p (n h d) -> p n h d", h=2, d=XPAD)[:, :, h, :]
                nc.vector.tensor_tensor(Vc[r, :, h * XPAD:(h + 1) * XPAD], pair(ps[6][r, :]), pair(vb[r, 1, :]), ALU.add).then_inc(s["vcev"], 1)

            def shifted(u):
                dve.wait_ge(s["sps"], GROUPS * b + u + 1)
                for a, lo, hi, n in psum_parts():
                    nc.vector.tensor_reduce(mx[:, u % 2, lo:hi], a, AX_X, ALU.max).then_inc(s["max"], 1)
                dve.wait_ge(s["max"], 4 * GROUPS * b + 4 * (u + 1))
                if u >= 2:
                    dve.wait_ge(s["tps"], 2 * GROUPS * b + 2 * (u - 1))
                for (a, lo, hi, n), d in zip(psum_parts(), sbuf_parts(Pb[u % 2])):
                    i = nc.vector.tensor_tensor(d, a, col(mx, u % 2, lo, hi, n), ALU.subtract)
                i.then_inc(s["sub"], 1)

            shifted(0)
            for u in range(GROUPS):
                if u + 1 < GROUPS:
                    shifted(u + 1)
                dve.wait_ge(s["exp"], GROUPS * b + u + 1)
                for a, lo, hi, n in parts(Pb[u % 2]):
                    nc.vector.tensor_reduce(sm[:, u % 2, lo:hi], a, AX_X, ALU.add).then_inc(s["sum"], 1)
                dve.wait_ge(s["sum"], 3 * GROUPS * b + 3 * (u + 1))
                nc.vector.reciprocal(rc[:, u % 2, :], sm[:, u % 2, :]).then_inc(s["rc"], 1)
            dve.wait_ge(s["wps"], b + 1)
            nc.vector.scalar_tensor_tensor(Z[:, bass.ds(b * T, T)], ps[7][:, 0:T], vec[:, 4:5], X[:, bass.ds(b * T, T)],
                                           ALU.add, ALU.add).then_inc(s["res"], 1)

    @block.gpsimd
    def _(pool):
        with pool.Fori(0, B) as b:
            for u in range(GROUPS):
                pool.wait_ge(s["rc"], GROUPS * b + u + 1)
                for a, lo, hi, n in parts(Pb[u % 2]):
                    nc.gpsimd.tensor_tensor(a, a, col(rc, u % 2, lo, hi, n), ALU.mult).then_inc(s["pn"], 1)

    @block.scalar
    def _(act):
        act.wait_ge(s["in"], NIN)
        with act.Fori(0, B) as b:
            act.wait_ge(s["kps"], b + 1)
            nc.scalar.activation(kT[:, :], ps[1][:, 0:T], ACT.Identity, bias=vec[:, 1:2]).then_inc(s["kev"], 1)
            act.wait_ge(s["kcps"], b + 1)
            nc.scalar.activation(kcT[:, 0:CTX], ps[3][:, 0:CTX], ACT.Identity, bias=vec[:, 3:4]).then_inc(s["kcev"], 1)
            act.wait_ge(s["qps"], b + 1)
            nc.scalar.activation(qT[:, :], ps[0][:, 0:T], ACT.Identity, bias=vec[:, 0:1]).then_inc(s["qev"], 1)
            act.wait_ge(s["qcps"], b + 1)
            nc.scalar.activation(qcT[:, :], ps[2][:, 0:T], ACT.Identity, bias=vec[:, 2:3]).then_inc(s["qcev"], 1)

            def exps(u):
                act.wait_ge(s["sub"], GROUPS * b + u + 1)
                nc.scalar.activation(Pb[u % 2][:, :], Pb[u % 2][:, :], ACT.Exp, scale=SCALE).then_inc(s["exp"], 1)

            exps(0)
            for u in range(GROUPS):
                if u + 1 < GROUPS:
                    exps(u + 1)
                for i in range(2):
                    act.wait_ge(s["tps"], 2 * GROUPS * b + 2 * u + i + 1)
                    if u:
                        act.wait_ge(s["yps"], GROUPS * b + u)
                    for c in range(2):
                        nc.scalar.copy(PT[i][:, c * HALF:(c + 1) * HALF], ps[4 + c][:, :]).then_inc(s["pev"], 1)
                act.wait_ge(s["yps"], GROUPS * b + u + 1)
                nc.scalar.copy(Y[:, u, :], ps[6][:, 0:T]).then_inc(s["yev"], 1)


def local_layers(nc, g, scope):
    ps, t, sem, X, X0 = g["ps"], g["t"], g["sem"], g["Z"], g["X"]
    ident, identb, eps = g["ident"], g["identb"], g["eps"]
    STEPS = DEPTH * B

    def sb(name, shape, dt=F32):
        return scope.enter_context(nc.sbuf_tensor(f"la_{name}", shape, dt))

    Wqkv = sb("Wqkv", [P, PAIRS, 3 * P])
    Wo = sb("Wo", [P, PAIRS, P])
    W1 = sb("W1", [P, 2 * INNER])
    W2 = sb("W2", [P, len(FC), P])
    vec = sb("vec", [P, 9])
    qks = sb("qks", [P, DEPTH, 2, 2 * LD])
    tc = sb("tc", [P, 2, TILES, 2 * P])
    tab = sb("tab", [P, DEPTH * 2 * HALF])
    mask = sb("mask", [P, TILES, 2 * SEG], BF16)
    xs = sb("xs", [P, T])
    V = sb("V", [P, 4, TILES, P])
    t1, t2, sq, qk = ([sb(f"{n}{i}", [P, HALF]) for i in range(2)] for n in ("t1", "t2", "sq", "qk"))
    ss, rn = ([sb(f"{n}{i}", [P, 8]) for i in range(2)] for n in ("ss", "rn"))
    qT = [sb(f"qT{i}", [P, T]) for i in range(2)]
    kz = [sb(f"kz{i}", [P, 2, T]) for i in range(2)]
    pr = [sb(f"pr{i}", [P, TILES * 2 * SEG]) for i in range(2)]
    mx, sm, rc = ([sb(f"{n}{i}", [P, 4]) for i in range(2)] for n in ("mx", "sm", "rc"))
    PT = [sb(f"PT{i}", [P, 2, T]) for i in range(2)]
    PW = [sb(f"PW{i}", [P, 2, WIN]) for i in range(2)]
    OT = sb("OT", [P, PAIRS, T])
    xf, xc, sqf = sb("xf", [P, T]), sb("xc", [P, T]), sb("sqf", [P, T])
    av, gt = sb("av", [P, len(FC), T]), sb("gt", [P, len(FC), T])

    per_pair = ["proj", "t1", "t2", "ss", "ssg", "sq", "vev", "ln", "rn", "rot", "qk", "tr", "tev", "sc", "max", "nmx", "exp",
                "rc", "pn", "pt", "ptev", "pwev", "pv", "otev"]
    per_step = ["xs", "wo", "x1", "xf", "mean", "xc", "sqf", "var", "lnv", "rstd", "xn", "xng", "hg", "av", "gb", "gelu", "hs", "w2", "x2"]
    s = {n: sem(f"la_{n}") for n in per_pair + per_step + ["in", "tabs", "zero", "x0", "wo_in", "ff_in"]}
    w_in = [sem(f"la_wqkv_in{p}") for p in range(PAIRS)]
    block = scope.enter_context(nc.Block())
    banks = g["psum"][:, 0:TILES * HALF].rearrange("p (t c) -> p t c", t=TILES)
    qk_banks, v_banks = banks[:, :, 0:2 * P], banks[:, :, 2 * P:3 * P]
    sc_banks = g["psum"][:, 3 * HALF:5 * HALF].rearrange("p (t c) -> p t c", t=TILES)[:, :, 0:2 * SEG] \
        .rearrange("p t (h k) -> p t h k", h=2)
    heads = lambda a: a.rearrange("p (h d) -> p h d", d=LD)
    seg = lambda a: a.rearrange("p (h k) -> p h k", k=SEG)
    bc = lambda a, n: a.rearrange("p (h o) -> p h o", o=1).broadcast_to([P, a.shape[1], n])

    def run(eng, slot):
        for p in range(PAIRS):
            slot(0, p, lambda d: p >= d, False)
        with eng.Fori(1, STEPS) as j:
            for p in range(PAIRS):
                slot(j, p, lambda d: True, True)
        for p in range(PAIRS):
            slot(STEPS, p, lambda d: p < d, True)

    @block.sync
    def _(sp):
        sp.dma_start(qks[:, :, :, :], t["la_qks"]).then_inc(s["in"], 16)
        sp.dma_start(tc[:, :, :, :], t["la_tc"]).then_inc(s["in"], 16)
        sp.dma_start(mask[:, :, :], t["la_mask"]).then_inc(s["in"], 16)

        def load(layer, pair_wait, wo_wait, x2_wait):
            for p in range(PAIRS):
                if pair_wait is not None:
                    sp.wait_ge(s["proj"], pair_wait + p)
                sp.dma_start(Wqkv[:, p, :], t["la_wqkv"][layer, :, p, :]).then_inc(w_in[p], 16)
            if wo_wait is not None:
                sp.wait_ge(s["wo"], wo_wait)
            sp.dma_start(Wo[:, :, :], t["la_wo"][layer]).then_inc(s["wo_in"], 16)
            if x2_wait is not None:
                sp.wait_ge(s["x2"], x2_wait)
            sp.dma_start(W1[:, :], t["la_w1"][layer]).then_inc(s["ff_in"], 16)
            sp.dma_start(W2[:, :, :], t["la_w2"][layer]).then_inc(s["ff_in"], 16)
            sp.dma_start(vec[:, :], t["la_vec"][layer]).then_inc(s["ff_in"], 16)

        load(0, None, None, None)
        with sp.Fori(1, DEPTH) as layer:
            load(layer, PAIRS * (B * layer - 1) + 1, B * layer, B * layer)

    @block.tensor
    def _(pe):
        pe.wait_ge(s["in"], 48)
        pe.wait_ge(s["zero"], 4)

        def slot(j, p, live, tail):
            k = PAIRS * j + p
            if live(0):
                if p == 0:
                    pe.wait_ge(s["xs"], 2 * j + 2)
                pe.wait_ge(w_in[p], 16 * (j // B) + 16)
                if live(1):
                    pe.wait_ge(s["t2"], k)
                    pe.wait_ge(s["vev"], k)
                for i in range(TILES):
                    o = nc.tensor.matmul(ps[i][:, 0:3 * P], xs[:, i * P:(i + 1) * P], Wqkv[:, p, :], start=True, stop=True)
                o.then_inc(s["proj"], 1)
            if tail and p == 3:
                pe.wait_ge(s["wo_in"], 16 * ((j - 1) // B) + 16)
                pe.wait_ge(s["otev"], PAIRS * j)
                for q in range(PAIRS):
                    o = nc.tensor.matmul(ps[6][:, 0:T], Wo[:, q, :], OT[:, q, :], start=(q == 0), stop=(q == PAIRS - 1))
                o.then_inc(s["wo"], 1)
            if live(1):
                pe.wait_ge(s["qk"], k)
                if live(2):
                    pe.wait_ge(s["tev"], 3 * (k - 1))
                q = qk[(p + 1) % 2]
                for i in range(TILES):
                    nc.tensor.transpose(ps[2][:, i * P:(i + 1) * P], q[:, 2 * P * i:2 * P * i + P], ident[:, :])
                    o = nc.tensor.transpose(ps[2][:, T + i * P:T + (i + 1) * P], q[:, 2 * P * i + P:2 * P * (i + 1)], ident[:, :])
                o.then_inc(s["tr"], 1)
            if tail and p == 4:
                pe.wait_ge(s["sqf"], j)
                nc.tensor.matmul(ps[6][:, 0:T], g["ones"][:, :], sqf[:, :], start=True, stop=True).then_inc(s["var"], 1)
            if tail and p == 5:
                hidden(j, 1)
            if live(3):
                pe.wait_ge(s["pn"], k - 2)
                if live(4):
                    pe.wait_ge(s["ptev"], k - 3)
                    pe.wait_ge(s["otev"], k - 3)
                pp = pr[(p + 1) % 2]
                for h in range(2):
                    for i in range(TILES):
                        c0 = (2 * i + h) * SEG + WIN
                        nc.tensor.transpose(ps[5][:, h * T + i * P:h * T + (i + 1) * P], pp[:, c0:c0 + P], ident[:, :])
                    c1 = (2 + h) * SEG + WIN
                    o = nc.tensor.transpose(ps[7][:, T + h * P:T + (h + 1) * P], pp[:, c1 - P:c1], ident[:, :])
                o.then_inc(s["pt"], 1)
            if live(1):
                pe.wait_ge(s["tev"], 3 * k)
                if live(2):
                    pe.wait_ge(s["exp"], k - 1)
                qq, kk = qT[(p + 1) % 2], kz[(p + 1) % 2]
                for i in range(TILES):
                    nc.tensor.matmul(ps[3 + i][:, 0:2 * SEG], identb[:, :], mask[:, i, :], start=True, stop=False, skip_group_check=True)
                nc.tensor.matmul(seg(ps[3][:, 0:2 * SEG])[:, :, WIN:], qq[:, 0:P], kk[:, :, 0:P], start=False, stop=True, skip_group_check=True)
                nc.tensor.matmul(seg(ps[4][:, 0:2 * SEG]), qq[:, P:T], kk[:, :, P - WIN:T], start=False, stop=True, skip_group_check=True).then_inc(s["sc"], 1)
            if tail and p == 7:
                pe.wait_ge(s["hs"], j)
                for c, (_, n) in enumerate(FC):
                    o = nc.tensor.matmul(ps[6][:, 0:T], W2[0:n, c, :], av[0:n, c, :], start=(c == 0), stop=(c == len(FC) - 1))
                o.then_inc(s["w2"], 1)
            if live(3):
                pe.wait_ge(s["ptev"], k - 2)
                pe.wait_ge(s["pwev"], k - 2)
                v = V[:, (p + 1) % 4, :, :]
                for h in range(2):
                    r = slice(h * LD, (h + 1) * LD)
                    pt = PT[(p + 1) % 2]
                    nc.tensor.matmul(ps[7][r, 0:P], v[:, 0, r], pt[:, h, 0:P], start=True, stop=True)
                    nc.tensor.matmul(ps[7][r, P:T], v[:, 1, r], pt[:, h, P:T], start=True, stop=False, skip_group_check=True)
                    o = nc.tensor.matmul(ps[7][r, P:P + WIN], v[:, 0, r], PW[(p + 1) % 2][:, h, :], start=False, stop=True, skip_group_check=True)
                o.then_inc(s["pv"], 1)
            if tail and p == 3:
                pe.wait_ge(s["xf"], 2 * j)
                nc.tensor.matmul(ps[6][:, 0:T], g["ones"][:, :], xf[:, :], start=True, stop=True).then_inc(s["mean"], 1)
            if tail and p == 4:
                hidden(j, 0)
            if tail and p == 5:
                hidden(j, 2)

        def hidden(j, c):
            f0, n = FC[c]
            if c == 0:
                pe.wait_ge(s["ff_in"], 48 * ((j - 1) // B) + 48)
                pe.wait_ge(s["xng"], j)
            else:
                pe.wait_ge(s["gb"], 3 * (j - 1) + c)
            nc.tensor.matmul(ps[6][0:n, 0:T], W1[:, f0:f0 + n], xc[:, :], start=True, stop=True)
            nc.tensor.matmul(ps[6][0:n, T:2 * T], W1[:, INNER + f0:INNER + f0 + n], xc[:, :], start=True, stop=True).then_inc(s["hg"], 1)

        run(pe, slot)

    @block.vector
    def _(dve):
        nc.vector.tensor_copy(X[:, :], X0[:, :]).then_inc(s["x0"], 1)
        nc.vector.memset(kz[0][:, :, :], 0.0).then_inc(s["zero"], 1)
        nc.vector.memset(kz[1][:, :, :], 0.0).then_inc(s["zero"], 1)
        nc.vector.memset(PW[0][:, :, :], 0.0).then_inc(s["zero"], 1)
        nc.vector.memset(PW[1][:, :, :], 0.0).then_inc(s["zero"], 1)
        nc.vector.memset(gt[:, :, :], 0.0).then_inc(s["zero"], 1)
        nc.vector.memset(av[:, :, :], 0.0).then_inc(s["zero"], 1)
        dve.wait_ge(s["in"], 48)
        for layer in range(DEPTH):
            for i in range(2):
                for q in range(2):
                    part = lambda a: a.rearrange("p (t q c) -> p t q c", t=TILES, q=2)[:, :, q, :]
                    o = nc.vector.tensor_tensor(part(tab[:, (2 * layer + i) * HALF:(2 * layer + i + 1) * HALF]), part(tc[:, i, :, :].rearrange("p t c -> p (t c)")),
                                                qks[:, layer, q:q + 1, :].broadcast_to([P, TILES, 2 * LD]), ALU.mult)
        o.then_inc(s["tabs"], 1)
        dve.wait_ge(s["x0"], 1)
        dve.wait_ge(s["zero"], 6)
        dve.wait_ge(s["tabs"], 1)

        def shift_in(dst, src, off, done):
            nc.vector.tensor_scalar(dst[0:64, :], src[0:64, bass.ds(off, T)], 1.0, None, ALU.mult).then_inc(done, 1)
            nc.vector.tensor_scalar(dst[64:P, 1:T], src[64:P, bass.ds(off, T - 1)], 1.0, None, ALU.mult).then_inc(done, 1)

        nc.vector.memset(xs[64:P, 0:1], 0.0)
        nc.vector.memset(xf[64:P, 0:1], 0.0)
        shift_in(xs, X, 0, s["xs"])

        def slot(j, p, live, tail):
            k = PAIRS * j + p
            a = p % 2
            off = ((j - 1) % B) * T if tail else 0
            if tail and p == 4:
                dve.wait_ge(s["mean"], j)
                nc.vector.tensor_tensor(xc[:, :], xf[:, :], ps[6][:, 0:T], ALU.subtract).then_inc(s["xc"], 1)
            if tail and p == 5:
                values(j, 0)
            if tail and p == 6:
                values(j, 2)
            if live(0):
                dve.wait_ge(s["proj"], k + 1)
                if live(2):
                    dve.wait_ge(s["qk"], k - 1)
                tiles = lambda x: x.rearrange("p (t c) -> p t c", t=TILES)
                nc.vector.tensor_tensor(tiles(t1[a][:, :]), qk_banks, tiles(tab[:, bass.ds(j // B * 2 * HALF, HALF)]), ALU.mult).then_inc(s["t1"], 1)
                nc.vector.tensor_tensor(tiles(t2[a][:, :]), qk_banks, tiles(tab[:, bass.ds(j // B * 2 * HALF + HALF, HALF)]), ALU.mult).then_inc(s["t2"], 1)
            if live(0) and p == PAIRS - 1:
                shift_in(xs, X, ((j + 1) % B) * T, s["xs"])
            if live(2):
                dve.wait_ge(s["exp"], k - 1)
                nc.vector.reciprocal(rc[a][:, :], sm[a][:, :]).then_inc(s["rc"], 1)
            if tail and p == 3:
                dve.wait_ge(s["wo"], j)
                nc.vector.tensor_tensor(X[:, bass.ds(off, T)], X[:, bass.ds(off, T)], ps[6][:, 0:T], ALU.add).then_inc(s["x1"], 1)
                dve.wait_ge(s["x1"], j)
                shift_in(xf, X, off, s["xf"])
            if live(3):
                dve.wait_ge(s["pt"], k - 2)
                if live(5):
                    dve.wait_ge(s["pv"], k - 4)
                nc.vector.tensor_copy(PT[(p + 1) % 2][:, :, :].rearrange("p h t -> p (h t)"), ps[5][:, :]).then_inc(s["ptev"], 1)
            if tail and p == 4:
                dve.wait_ge(s["rstd"], j)
                nc.vector.tensor_tensor(xc[:, :], xc[:, :], sqf[:, :], ALU.mult).then_inc(s["xn"], 1)
                dve.wait_ge(s["xn"], j)
                dve.wait_ge(s["ff_in"], 48 * ((j - 1) // B) + 48)
                nc.vector.tensor_scalar(xc[:, :], xc[:, :], vec[:, 7:8], vec[:, 8:9], ALU.mult, ALU.add).then_inc(s["xng"], 1)
            if tail and p == 5:
                values(j, 1)
            if live(0):
                dve.wait_ge(s["sq"], k + 1)
                nc.vector.tensor_reduce(ss[a][:, :], heads(sq[a][:, :]), AX_X, ALU.add).then_inc(s["ss"], 1)
                dve.wait_ge(s["ss"], k + 1)
                nc.vector.tensor_scalar(ss[a][:, :], ss[a][:, :], 1e-24, None, ALU.max).then_inc(s["ssg"], 1)
            if live(1):
                b = (p + 1) % 2
                dve.wait_ge(s["sc"], k)
                nc.vector.tensor_reduce(mx[b][:, :].rearrange("p (t h) -> p t h", t=TILES), sc_banks, AX_X, ALU.max).then_inc(s["max"], 1)
                dve.wait_ge(s["max"], k)
                nc.vector.tensor_scalar(mx[b][:, :], mx[b][:, :], -QK_SCALE, None, ALU.mult).then_inc(s["nmx"], 1)
            if tail and p == 7:
                dve.wait_ge(s["w2"], j)
                nc.vector.scalar_tensor_tensor(X[:, bass.ds(off, T)], ps[6][:, 0:T], vec[:, 6:7], X[:, bass.ds(off, T)],
                                               ALU.add, ALU.add).then_inc(s["x2"], 1)

        def values(j, c):
            n = FC[c][1]
            dve.wait_ge(s["hg"], 3 * (j - 1) + c + 1)
            nc.vector.tensor_scalar(av[0:n, c, :], ps[6][0:n, 0:T], vec[0:n, c:c + 1], None, ALU.add).then_inc(s["av"], 1)

        run(dve, slot)
        dve.wait_ge(s["x2"], STEPS)
        nc.vector.tensor_tensor(X[:, :], X[:, :], X0[:, :], ALU.add)

    @block.gpsimd
    def _(pool):
        def slot(j, p, live, tail):
            k = PAIRS * j + p
            a = p % 2
            if live(2):
                pool.wait_ge(s["rc"], k - 1)
                nc.gpsimd.tensor_tensor(seg(pr[a][:, :]), seg(pr[a][:, :]), bc(rc[a][:, :], SEG), ALU.mult).then_inc(s["pn"], 1)
            if tail and p == 7:
                pool.wait_ge(s["gelu"], j)
                pool.wait_ge(s["av"], 3 * j)
                nc.gpsimd.tensor_tensor(av[:, :, :], av[:, :, :], gt[:, :, :], ALU.mult).then_inc(s["hs"], 1)
            if live(0):
                pool.wait_ge(s["t2"], k + 1)
                half = lambda x: x[:, :].rearrange("p (h u d) -> p h u d", u=2, d=LD // 2)
                nc.gpsimd.tensor_tensor(half(t1[a]), half(t1[a]), half(t2[a])[:, :, ::-1, :], ALU.add).then_inc(s["rot"], 1)
                pool.wait_ge(s["rot"], k + 1)
                pool.wait_ge(s["rn"], k + 1)
                if live(2):
                    pool.wait_ge(s["tr"], k - 1)
                nc.gpsimd.tensor_tensor(heads(qk[a][:, :]), heads(t1[a][:, :]), bc(rn[a][:, :], LD), ALU.mult).then_inc(s["qk"], 1)

        run(pool, slot)

    @block.scalar
    def _(act):
        act.wait_ge(s["zero"], 6)

        def slot(j, p, live, tail):
            k = PAIRS * j + p
            a = p % 2
            if live(2):
                act.wait_ge(s["nmx"], k - 1)
                if live(4):
                    act.wait_ge(s["pt"], k - 3)
                for i in range(TILES):
                    for h in range(2):
                        n = 2 * i + h
                        o = nc.scalar.activation(pr[a][:, n * SEG:(n + 1) * SEG], ps[3 + i][:, h * SEG:(h + 1) * SEG], ACT.Exp,
                                                 scale=QK_SCALE, bias=mx[a][:, n:n + 1], accum_out=sm[a][:, n:n + 1])
                o.then_inc(s["exp"], 1)
            if tail and p == 4:
                act.wait_ge(s["xc"], j)
                nc.scalar.activation(sqf[:, :], xc[:, :], ACT.Square).then_inc(s["sqf"], 1)
            if tail and p == 5:
                gates(j, 0)
            if tail and p == 6:
                gates(j, 2)
            if live(1):
                b = (p + 1) % 2
                act.wait_ge(s["tr"], k)
                if live(3):
                    act.wait_ge(s["sc"], k - 2)
                nc.scalar.copy(qT[b][:, :], ps[2][:, 0:T]).then_inc(s["tev"], 1)
                for h in range(2):
                    r = slice(h * LD, (h + 1) * LD)
                    nc.scalar.copy(kz[b][r, h, :], ps[2][r, T:]).then_inc(s["tev"], 1)
            if tail and p == 4:
                act.wait_ge(s["var"], j)
                nc.scalar.activation(sqf[:, :], ps[6][:, 0:T], ACT.Ln, bias=eps[:, 0:1]).then_inc(s["lnv"], 1)
                act.wait_ge(s["lnv"], j)
                nc.scalar.activation(sqf[:, :], sqf[:, :], ACT.Exp, scale=-0.5).then_inc(s["rstd"], 1)
            if live(0):
                act.wait_ge(s["t2"], k + 1)
                if live(2):
                    act.wait_ge(s["ss"], k - 1)
                nc.scalar.activation(sq[a][:, :].rearrange("p (t c) -> p t c", t=TILES), qk_banks, ACT.Square).then_inc(s["sq"], 1)
                if live(4):
                    act.wait_ge(s["pv"], k - 3)
                nc.scalar.copy(V[:, p % 4, :, :], v_banks).then_inc(s["vev"], 1)
            if live(3):
                act.wait_ge(s["pt"], k - 2)
                if live(5):
                    act.wait_ge(s["pv"], k - 4)
                nc.scalar.copy(PW[(p + 1) % 2][96:P, :, :], ps[7][96:P, T:].rearrange("p (h q) -> p h q", h=2)[:, :, 0:WIN]).then_inc(s["pwev"], 1)
            if tail and p == 5:
                gates(j, 1)
            if live(0):
                act.wait_ge(s["ssg"], k + 1)
                nc.scalar.activation(rn[a][:, :], ss[a][:, :], ACT.Ln, scale=SS_SCALE).then_inc(s["ln"], 1)
                act.wait_ge(s["ln"], k + 1)
                nc.scalar.activation(rn[a][:, :], rn[a][:, :], ACT.Exp, scale=-0.5, bias=eps[:, 2:3]).then_inc(s["rn"], 1)
            if tail and p == 6:
                act.wait_ge(s["gb"], 3 * j)
                nc.scalar.activation(gt[:, :, :], gt[:, :, :], ACT.Gelu).then_inc(s["gelu"], 1)
                nc.scalar.preload_act_table_set(LN_EXP)
            if live(3):
                act.wait_ge(s["pv"], k - 2)
                if tail and p == 3:
                    act.wait_ge(s["wo"], j)
                nc.scalar.copy(OT[:, (p - 3) % PAIRS, :], ps[7][:, 0:T]).then_inc(s["otev"], 1)

        def gates(j, c):
            n = FC[c][1]
            act.wait_ge(s["av"], 3 * (j - 1) + c + 1)
            nc.scalar.activation(gt[0:n, c, :], ps[6][0:n, T:2 * T], ACT.Identity, bias=vec[0:n, 3 + c:4 + c]).then_inc(s["gb"], 1)

        run(act, slot)


def _constants():
    import numpy as np

    bf16 = lambda a: (np.ascontiguousarray(a, np.float32).view(np.uint32) >> 16).astype(np.uint16)
    i = np.arange(P)
    c = {"ident": np.eye(P, dtype=np.float32), "identb": bf16(np.eye(P)),
         "ones": np.full((P, P), 1.0 / P, np.float32),
         "blk": np.where(i[:, None] // RD == i[None, :] // RD, 1.0 / RD, 0.0).astype(np.float32)}
    eps = np.zeros((P, 4), np.float32)
    eps[:, 0], eps[:, 1], eps[:, 2] = LN_EPS, GN_EPS, 0.5 * np.log(SS_SCALE)
    c["eps"] = eps
    m = np.zeros((P, LEVELS, P), np.int32)
    src, tgt = i[:, None], i[None, :]
    m[:, 0] = src == tgt
    for lv in range(LEVELS - 1):
        h = 1 << lv
        m[:, lv + 1] = (src // (2 * h) == tgt // (2 * h)) & (src % (2 * h) < h) & (tgt % (2 * h) >= h)
    c["tm_masks"] = m
    c["xa_hm"] = (i[:, None] // XD == np.arange(XH)[None, :]).astype(np.float32)
    cut = np.where(i[None, :] > i[:, None], -BIG, 0.0)
    causal = np.zeros((P, 2, 2 * T))
    causal[:, 0] = np.tile(cut, (1, 4))
    causal[:, 1] = np.tile(np.concatenate([np.zeros((P, P)), cut], 1), (1, 2))
    c["xa_causal"] = bf16(causal)
    q, k = i[:, None], np.arange(SEG)[None, :] - WIN
    near = (k <= q) & (q - k <= WIN)
    mask = np.zeros((P, TILES, 2, SEG))
    for tile in range(TILES):
        mask[:, tile] = np.where(near & (k + tile * P >= 0), 0.0, -BIG)[:, None, :]
    c["la_mask"] = bf16(mask.reshape(P, TILES, 2 * SEG))
    half = np.arange(0, LD, 2, dtype=np.float64)
    pos = np.arange(T, dtype=np.float64)
    freqs = (pos[:, None] * (1.0 / 10000.0 ** (half / LD))[None, :])
    scale = ((half + 0.4 * LD) / (1.4 * LD))[None, :] ** ((pos - T // 2) / (WIN // 2))[:, None]
    tc = np.zeros((2, T, 2, 2, 2, LD // 2))
    for n, sc in enumerate((scale, 1.0 / scale)):
        tc[0, :, n] = (np.cos(freqs) * sc)[:, None, None, :]
        tc[1, :, n, :, 0] = (np.sin(freqs) * sc)[:, None, :]
        tc[1, :, n, :, 1] = -(np.sin(freqs) * sc)[:, None, :]
    c["la_tc"] = tc.reshape(2, TILES, P, 2 * P).transpose(2, 0, 1, 3).astype(np.float32)
    return c


def _layout(a):
    import numpy as np

    f = lambda n: np.asarray(a[n])
    cols = lambda *names: np.stack([f(n).reshape(P) for n in names], 1)
    d = {"xT": f("x").reshape(N, P).T}
    tm = "L0_attn_"
    d["tm_vec"] = cols(*(tm + n for n in ("time_maa_x", "time_maa_w", "time_maa_k", "time_maa_v", "time_maa_r", "time_decay",
                                          "time_faaaa", "ln_w", "ln_b")))
    d["tm_w"] = np.concatenate([f(tm + "time_maa_w1"), f(tm + "time_maa_w2").reshape(P, P), f(tm + "W_r"), f(tm + "W_k"),
                                f(tm + "W_v"), f(tm + "W_o"), f(tm + "time_decay_w1")], 1)
    d["tm_dw2"] = f(tm + "time_decay_w2")
    xa = "L0_xattn_"

    def padded(w):
        out = np.zeros((w.shape[0], XH, XPAD), np.float32)
        out[:, :, :XD] = w.reshape(-1, XH, XD)
        return out.reshape(-1, XH * XPAD)

    wp = padded(f(xa + "Wp").T).T.reshape(XH // HG, P, P).transpose(1, 0, 2).reshape(P, -1)
    d["xa_w"] = np.concatenate([f(xa + "Wq"), f(xa + "Wk"), f(xa + "Wcq"), padded(f(xa + "Wv")), wp], 1)
    d["xa_cw"] = np.concatenate([f(xa + "Wck"), padded(f(xa + "Wcv"))], 1)
    d["xa_vec"] = cols(*(xa + n for n in ("bq", "bk", "bcq", "bck", "bp")))
    d["xa_vb"] = np.broadcast_to(np.stack([padded(f(xa + n)[None])[0] for n in ("bv", "bcv")]), (P, 2, XH * XPAD))
    ct = f("ctx_512").transpose(2, 0, 1)
    d["ctxT"] = np.concatenate([ct, ct], 2).reshape(CC, B * P)
    la = "L0_ffn_"
    d["la_wqkv"] = f(la + "Wqkv").reshape(DEPTH, P, 3, PAIRS, P).transpose(0, 1, 3, 2, 4).reshape(DEPTH, P, PAIRS, 3 * P)
    d["la_wo"] = f(la + "Wo").reshape(DEPTH, PAIRS, P, P).transpose(0, 2, 1, 3)
    d["la_w1"] = f(la + "W1")
    w2 = np.zeros((DEPTH, len(FC) * P, P), np.float32)
    w2[:, :INNER] = f(la + "W2")
    d["la_w2"] = w2.reshape(DEPTH, len(FC), P, P).transpose(0, 2, 1, 3)
    vec = np.zeros((DEPTH, 9, P), np.float32)
    b1 = f(la + "b1")
    for c, (f0, n) in enumerate(FC):
        vec[:, c, :n], vec[:, 3 + c, :n] = b1[:, f0:f0 + n], b1[:, INNER + f0:INNER + f0 + n]
    vec[:, 6], vec[:, 7], vec[:, 8] = f(la + "b2"), f(la + "ln_g"), f(la + "ln_b")
    d["la_vec"] = vec.transpose(0, 2, 1)
    qk = np.stack([f(la + "q_scale"), f(la + "k_scale")], 1)
    d["la_qks"] = np.broadcast_to(np.concatenate([qk, qk], 2), (P, DEPTH, 2, 2 * LD))
    return d


def kernel(**inputs):
    import numpy as np
    import concourse.bacc as bacc
    from concourse.bass_utils import run_bass_kernel_spmd

    nc = bacc.Bacc("TRN2", target_bir_lowering=False, num_devices=1)
    arrays = {n: np.ascontiguousarray(a) for n, a in {**_layout(inputs), **_constants()}.items()}
    t = {n: nc.dram_tensor(f"in_{n}", a.shape, mybir.dt.from_np(a.dtype), kind="ExternalInput").ap() for n, a in arrays.items()}
    for n in ("identb", "xa_causal", "la_mask"):
        t[n] = t[n].bitcast(BF16)
    t["out"] = nc.dram_tensor("out", (P, N), F32, kind="ExternalOutput").ap()
    build(nc, t)
    r = run_bass_kernel_spmd(nc, [{f"in_{n}": a for n, a in arrays.items()}], core_ids=[0])
    return np.ascontiguousarray(r.results[0]["out"].T).reshape(B, T, P)
```

```python
from contextlib import ExitStack

import concourse.bass as bass
from concourse import mybir

F32 = mybir.dt.float32
BF16 = mybir.dt.bfloat16
I32 = mybir.dt.int32
ALU = mybir.AluOpType
ACT = mybir.ActivationFunctionType
AX_X = mybir.AxisListType.X

P = 128
B, T = 4, 256
N = B * T
TILES = T // P
HALF = 512

RH, RD = 2, 64
LEVELS = 8
GN_EPS, LN_EPS = 0.00064, 1e-05
XH, XD, CTX, CC = 16, 8, 64, 64
XPAD = 32
HG = 4
DEPTH, LH, LD, WIN = 6, 16, 64, 32
PAIRS = LH // 2
SEG = WIN + P
INNER = 341
FC = [(0, 128), (128, 128), (256, 85)]
QK_SCALE = 8.0
BIG = 1.0e30
LN_EXP = "natural_log_exp_and_others"
SS_SCALE = float(2 ** 20)


def build(nc, t):
    with ExitStack() as ctx:
        def sb(name, shape, dt=F32):
            return ctx.enter_context(nc.sbuf_tensor(name, shape, dt))

        def sem(name):
            return ctx.enter_context(nc.semaphore(name))

        psum = ctx.enter_context(nc.psum_tensor("psum", [P, 8 * HALF], F32))
        ps = [psum[:, i * HALF:(i + 1) * HALF] for i in range(8)]
        g = {
            "sb": sb, "sem": sem, "ps": ps, "psum": psum, "t": t, "ctx": ctx,
            "ident": sb("identity", [P, P]), "identb": sb("identity_bf16", [P, P], BF16),
            "ones": sb("channel_mean", [P, P]), "blk": sb("head_mean", [P, P]), "eps": sb("epsilons", [P, 4]),
            "X": sb("X", [P, N]), "Z": sb("Z", [P, N]),
        }
        g["xa"] = cross_attention_inputs(nc, g)
        with ExitStack() as scope:
            time_mix(nc, g, scope)
        layer_norm(nc, g, "ln1", g["Z"], g["X"])
        g["la"] = local_layers_inputs(nc, g)
        with ExitStack() as scope:
            cross_attention(nc, g, scope)
        layer_norm(nc, g, "ln2", g["Z"], g["X"])
        with ExitStack() as scope:
            local_layers(nc, g, scope)
        layer_norm(nc, g, "ln3", g["Z"], g["X"], out=t["out"])


def layer_norm(nc, g, name, src, dst, out=None):
    ps = g["ps"]
    with ExitStack() as scope:
        xc = scope.enter_context(nc.sbuf_tensor(f"{name}_xc", [P, N], F32))
        sq = scope.enter_context(nc.sbuf_tensor(f"{name}_sq", [P, N], F32))
        names = ["mean", "centred", "squared", "var", "logvar", "rstd", "normed", "stored"]
        s = {n: g["sem"](f"{name}_{n}") for n in names}
        block = scope.enter_context(nc.Block())
        col = [slice(c * T, (c + 1) * T) for c in range(B)]

        @block.tensor
        def _(pe):
            for c in range(B):
                nc.tensor.matmul(ps[c][:, 0:T], g["ones"][:, :], src[:, col[c]], start=True, stop=True).then_inc(s["mean"], 1)
            for c in range(B):
                pe.wait_ge(s["squared"], c + 1)
                nc.tensor.matmul(ps[B + c][:, 0:T], g["ones"][:, :], sq[:, col[c]], start=True, stop=True).then_inc(s["var"], 1)

        @block.vector
        def _(dve):
            for c in range(B):
                dve.wait_ge(s["mean"], c + 1)
                nc.vector.tensor_tensor(xc[:, col[c]], src[:, col[c]], ps[c][:, 0:T], ALU.subtract).then_inc(s["centred"], 1)
            for c in range(B):
                dve.wait_ge(s["centred"], c + 1)
                dve.wait_ge(s["rstd"], c + 1)
                nc.vector.tensor_tensor(dst[:, col[c]], xc[:, col[c]], sq[:, col[c]], ALU.mult).then_inc(s["normed"], 1)

        @block.scalar
        def _(act):
            for c in range(B):
                act.wait_ge(s["centred"], c + 1)
                nc.scalar.activation(sq[:, col[c]], xc[:, col[c]], ACT.Square).then_inc(s["squared"], 1)
            for c in range(B):
                act.wait_ge(s["var"], c + 1)
                nc.scalar.activation(sq[:, col[c]], ps[B + c][:, 0:T], ACT.Ln, bias=g["eps"][:, 0:1]).then_inc(s["logvar"], 1)
            for c in range(B):
                act.wait_ge(s["logvar"], c + 1)
                nc.scalar.activation(sq[:, col[c]], sq[:, col[c]], ACT.Exp, scale=-0.5).then_inc(s["rstd"], 1)

        @block.sync
        def _(sp):
            if out is not None:
                for c in range(B):
                    sp.wait_ge(s["normed"], c + 1)
                    sp.dma_start(out[:, col[c]], dst[:, col[c]]).then_inc(s["stored"], 16)
                sp.wait_ge(s["stored"], 16 * B)


def time_mix(nc, g, scope):
    ps, t, sem = g["ps"], g["t"], g["sem"]

    def sb(name, shape, dt=F32):
        return scope.enter_context(nc.sbuf_tensor(f"tm_{name}", shape, dt))

    x = sb("x", [P, N])
    vec = sb("vec", [P, 9])
    wts = sb("wts", [P, 5 * P + 64])
    w2 = sb("w2", [P, 4, P])
    dw2 = sb("dw2", [64, P])
    masks = sb("masks", [P, LEVELS, P], I32)
    xx = sb("xx", [P, N])
    mixed = sb("mixed", [P, 4, N])
    m = sb("m", [P, N])
    R2 = sb("R2", [P, RH, N])
    K = sb("K", [P, N])
    V = sb("V", [P, N])
    w = sb("w", [P, N])
    bp = [w, sb("bp1", [P, N // 2]), sb("bp2", [P, N // 4])]
    pre = sb("pre", [P, N])
    suf = sb("suf", [P, N])
    rp = [sb(f"rp{i}", [P, RH, N]) for i in range(2)]
    kp = [sb(f"kp{i}", [P, N]) for i in range(2)]
    S = sb("S", [P, 4 * HALF])
    SX = sb("SX", [P, 2 * HALF])
    Y = sb("Y", [P, N])
    yc = sb("yc", [P, N])
    sq = sb("sq", [P, N])
    W = {n: wts[:, i * P:(i + 1) * P] for i, n in enumerate(["w1", "r", "k", "v", "o"])}
    dw1 = wts[:, 5 * P:5 * P + 64]
    col = [slice(c * HALF, (c + 1) * HALF) for c in range(2)]
    bt = lambda a: a[:, :].rearrange("p (b t) -> p b t", b=B)
    halves = lambda a, m: a[:, :].rearrange("p (n h m) -> p n h m", h=2, m=m)

    names = ["x_in", "vec_in", "in", "consts", "prep", "xx", "xxx", "m1", "mt", "m2", "mulx", "addx", "rps", "kps", "vps", "lps", "rev", "kev",
             "vev", "lev", "dps", "dev", "wev", "ku", "bpr", "pre", "suf", "kpr", "rpr", "gps", "gcp", "xev", "yps", "yev",
             "mean", "centred", "squared", "var", "logvar", "rstd", "yn", "yna", "ops"]
    s = {n: sem(f"tm_{n}") for n in names}
    block = scope.enter_context(nc.Block())

    @block.sync
    def _(sp):
        sp.dma_start(x[:, :], t["xT"]).then_inc(s["x_in"], 16)
        sp.dma_start(vec[:, :], t["tm_vec"]).then_inc(s["vec_in"], 16)
        sp.dma_start(wts[:, :], t["tm_w"]).then_inc(s["in"], 16)
        sp.dma_start(w2[:, :, :], t["tm_w2"]).then_inc(s["in"], 16)
        sp.dma_start(dw2[:, :], t["tm_dw2"]).then_inc(s["in"], 16)
        sp.dma_start(masks[:, :, :], t["tm_masks"]).then_inc(s["consts"], 16)
        sp.dma_start(g["ident"][:, :], t["ident"]).then_inc(s["consts"], 16)
        sp.dma_start(g["identb"][:, :], t["identb"]).then_inc(s["consts"], 16)
        sp.dma_start(g["ones"][:, :], t["ones"]).then_inc(s["consts"], 16)
        sp.dma_start(g["blk"][:, :], t["blk"]).then_inc(s["consts"], 16)
        sp.dma_start(g["eps"][:, :], t["eps"]).then_inc(s["consts"], 16)
        for dst, src in g["xa"]["loads"]:
            sp.dma_start(dst, t[src]).then_inc(g["xa"]["in"], 16)

    NCONST = 6 * 16

    @block.gpsimd
    def _(pool):
        for f in range(4):
            pool.wait_ge(s["mulx"], 2 * (f + 1))
            nc.gpsimd.tensor_tensor(mixed[:, f, :], mixed[:, f, :], x[:, :], ALU.add).then_inc(s["addx"], 1)
        pool.wait_ge(s["kev"], 2)
        for lv in range(1, LEVELS):
            pool.wait_ge(s["suf"], lv)
            if lv >= 2:
                pool.wait_ge(s["gps"], lv)
            left = lambda a: a[:, :] if lv <= 2 else halves(a, 1 << lv)[:, :, 0, :]
            nc.gpsimd.tensor_tensor(left(kp[lv % 2]), left(K), left(suf), ALU.mult).then_inc(s["kpr"], 1)

    @block.vector
    def _(dve):
        nc.vector.memset(pre[:, :], 1.0).then_inc(s["prep"], 1)
        dve.wait_ge(s["x_in"], 16)
        nc.vector.tensor_tensor(bt(xx)[:, :, 1:], bt(x)[:, :, :T - 1], bt(x)[:, :, 1:], ALU.subtract).then_inc(s["xx"], 1)
        nc.vector.tensor_scalar(bt(xx)[:, :, 0:1], bt(x)[:, :, 0:1], -1.0, None, ALU.mult).then_inc(s["xx"], 1)
        dve.wait_ge(s["xx"], 2)
        dve.wait_ge(s["vec_in"], 16)
        nc.vector.scalar_tensor_tensor(yc[:, :], xx[:, :], vec[:, 0:1], x[:, :], ALU.mult, ALU.add).then_inc(s["xxx"], 1)
        nc.vector.memset(R2[:, :, :], 0.0).then_inc(s["prep"], 1)
        nc.vector.memset(S[:, :], 0.0).then_inc(s["prep"], 1)
        nc.vector.memset(suf[:, :], 1.0).then_inc(s["prep"], 1)
        for f in range(4):
            for c in range(2):
                dve.wait_ge(s["m2"], 2 * f + c + 1)
                nc.vector.scalar_tensor_tensor(mixed[:, f, col[c]], ps[2 * f + c][:, :], vec[:, 1 + f:2 + f], xx[:, col[c]],
                                               ALU.add, ALU.mult).then_inc(s["mulx"], 1)
        dve.wait_ge(s["kev"], 2)
        nc.vector.tensor_scalar(kp[0][:, :], K[:, :], vec[:, 6:7], None, ALU.mult).then_inc(s["ku"], 1)
        dve.wait_ge(s["consts"], NCONST)

        def select(step):
            dve.wait_ge(s["gps"], step + 1)
            if step:
                dve.wait_ge(s["gcp"], step)
            h = 1 << (step - 1)
            right = lambda a: a.rearrange("p (n b h m) -> p n b h m", b=P // (2 * h), h=2, m=h)[:, :, :, 1, :]
            mask = masks[:, step, :].rearrange("p (n b h m) -> p n b h m", n=1, b=P // (2 * h), h=2, m=h)[:, :, :, 1, :]
            for c in range(2):
                for q in range(2):
                    i = nc.vector.copy_predicated(right(S[:, (2 * c + q) * HALF:(2 * c + q + 1) * HALF]),
                                                  mask.broadcast_to([P, 4, P // (2 * h), h]),
                                                  ps[4 * (step % 2) + c][:, q * 2 * P:(q + 1) * 2 * P].rearrange("p (n b m) -> p n b m", n=4, m=h))
            i.then_inc(s["gcp"], 1)

        def diagonal():
            dve.wait_ge(s["gps"], 1)
            for h in range(4):
                i = nc.vector.copy_predicated(S[:, h * HALF:(h + 1) * HALF].rearrange("p (n t) -> p n t", t=P),
                                              masks[:, 0:1, :].broadcast_to([P, 4, P]), ps[h][:, :].rearrange("p (n t) -> p n t", t=P))
            i.then_inc(s["gcp"], 1)

        dve.wait_ge(s["wev"], 2)
        dve.wait_ge(s["prep"], 4)
        dve.wait_ge(s["rev"], 4)
        for lv in range(1, LEVELS):
            mm = 1 << (lv - 1)
            whole = bp[0] if lv == 1 else bp[1 + (lv - 2) % 2]
            n = N // (2 * mm)
            wv = whole[:, :2 * n].rearrange("p (n h) -> p n h", h=2)
            if lv >= 2:
                dve.wait_ge(s["bpr"], lv - 1)
                dve.wait_ge(s["kpr"], lv - 1)
                dve.wait_ge(s["rpr"], lv - 1)
                dve.wait_ge(s["suf"], lv - 1)
            nc.vector.tensor_tensor(halves(suf, mm)[:, :, 0, :], halves(suf, mm)[:, :, 0, :],
                                    wv[:, :, 1:2].broadcast_to([P, n, mm]), ALU.mult).then_inc(s["suf"], 1)
            nc.vector.tensor_tensor(halves(pre, mm)[:, :, 1, :], halves(pre, mm)[:, :, 1, :],
                                    wv[:, :, 0:1].broadcast_to([P, n, mm]), ALU.mult).then_inc(s["pre"], 1)
            nxt = bp[1 + (lv - 1) % 2]
            nc.vector.tensor_tensor(nxt[:, :n].rearrange("p (n o) -> p n o", o=1), wv[:, :, 0:1], wv[:, :, 1:2],
                                    ALU.mult).then_inc(s["bpr"], 1)
            dve.wait_ge(s["pre"], lv)
            if lv >= 3:
                dve.wait_ge(s["gps"], lv)
            right = lambda a: a.rearrange("p o (n h m) -> p o n h m", h=2, m=2 * mm)[:, :, :, 1, :]
            for h in range(RH):
                i = nc.vector.tensor_tensor(right(rp[lv % 2][:, h:h + 1, :])[:, 0], right(R2[:, h:h + 1, :])[:, 0],
                                            halves(pre, 2 * mm)[:, :, 1, :], ALU.mult)
            i.then_inc(s["rpr"], 1)
            if lv == 1:
                diagonal()
            else:
                select(lv - 1)
        select(LEVELS - 1)
        for c in range(2):
            dve.wait_ge(s["yev"], c + 1)
            dve.wait_ge(s["mean"], c + 1)
            nc.vector.tensor_tensor(yc[:, col[c]], Y[:, col[c]], ps[c][:, :], ALU.subtract).then_inc(s["centred"], 1)
        for c in range(2):
            dve.wait_ge(s["centred"], c + 1)
            dve.wait_ge(s["rstd"], c + 1)
            nc.vector.tensor_tensor(yc[:, col[c]], yc[:, col[c]], sq[:, col[c]], ALU.mult).then_inc(s["yn"], 1)
            dve.wait_ge(s["yn"], c + 1)
            nc.vector.tensor_scalar(yc[:, col[c]], yc[:, col[c]], vec[:, 7:8], vec[:, 8:9], ALU.mult, ALU.add).then_inc(s["yna"], 1)
        for c in range(2):
            dve.wait_ge(s["ops"], c + 1)
            nc.vector.tensor_tensor(g["Z"][:, col[c]], x[:, col[c]], ps[4 + c][:, :], ALU.add)

    @block.scalar
    def _(act):
        for c in range(2):
            act.wait_ge(s["m1"], c + 1)
            nc.scalar.activation(m[:, col[c]], ps[c][:, :], ACT.Tanh).then_inc(s["mt"], 1)
        for c in range(2):
            act.wait_ge(s["lps"], c + 1)
            nc.scalar.activation(m[0:64, col[c]], ps[c][0:64, :], ACT.Tanh).then_inc(s["lev"], 1)
        for c in range(2):
            act.wait_ge(s["kps"], c + 1)
            nc.scalar.copy(K[:, col[c]], ps[2 + c][:, :]).then_inc(s["kev"], 1)
        for c in range(2):
            act.wait_ge(s["dps"], c + 1)
            nc.scalar.activation(w[:, col[c]], ps[c][:, :], ACT.Exp, bias=vec[:, 5:6]).then_inc(s["dev"], 1)
            act.wait_ge(s["dev"], c + 1)
            nc.scalar.activation(w[:, col[c]], w[:, col[c]], ACT.Exp, scale=-1.0).then_inc(s["wev"], 1)
        for c in range(2):
            act.wait_ge(s["vps"], c + 1)
            nc.scalar.copy(V[:, col[c]], ps[4 + c][:, :]).then_inc(s["vev"], 1)
        act.wait_ge(s["prep"], 2)
        for c in range(2):
            act.wait_ge(s["rps"], c + 1)
            for h in range(RH):
                r = slice(h * RD, (h + 1) * RD)
                nc.scalar.copy(R2[r, h, col[c]], ps[6 + c][r, :]).then_inc(s["rev"], 1)
        nc.scalar.preload_act_table_set(LN_EXP)
        act.wait_ge(s["gps"], LEVELS + 1)
        for c in range(2):
            nc.scalar.copy(SX[:, col[c]], ps[c][:, :]).then_inc(s["xev"], 1)
        for c in range(2):
            act.wait_ge(s["yps"], c + 1)
            nc.scalar.copy(Y[:, col[c]], ps[4 + c][:, :]).then_inc(s["yev"], 1)
        for c in range(2):
            act.wait_ge(s["centred"], c + 1)
            nc.scalar.activation(sq[:, col[c]], yc[:, col[c]], ACT.Square).then_inc(s["squared"], 1)
        for c in range(2):
            act.wait_ge(s["var"], c + 1)
            nc.scalar.activation(sq[:, col[c]], ps[2 + c][:, :], ACT.Ln, bias=g["eps"][:, 1:2]).then_inc(s["logvar"], 1)
        for c in range(2):
            act.wait_ge(s["logvar"], c + 1)
            nc.scalar.activation(sq[:, col[c]], sq[:, col[c]], ACT.Exp, scale=-0.5).then_inc(s["rstd"], 1)

    @block.tensor
    def _(pe):
        pe.wait_ge(s["in"], 48)
        pe.wait_ge(s["xxx"], 1)
        for c in range(2):
            nc.tensor.matmul(ps[c][:, :], W["w1"], yc[:, col[c]], start=True, stop=True).then_inc(s["m1"], 1)
        for f in range(4):
            for c in range(2):
                pe.wait_ge(s["mt"], c + 1 if f else 2)
                nc.tensor.matmul(ps[2 * f + c][:, :], w2[:, f, :], m[:, col[c]], start=True, stop=True).then_inc(s["m2"], 1)
        pe.wait_ge(s["addx"], 1)
        for c in range(2):
            nc.tensor.matmul(ps[c][0:64, :], dw1, mixed[:, 0, col[c]], start=True, stop=True).then_inc(s["lps"], 1)
        pe.wait_ge(s["addx"], 2)
        for c in range(2):
            nc.tensor.matmul(ps[2 + c][:, :], W["k"], mixed[:, 1, col[c]], start=True, stop=True).then_inc(s["kps"], 1)
        for c in range(2):
            pe.wait_ge(s["lev"], c + 1)
            nc.tensor.matmul(ps[c][:, :], dw2[:, :], m[0:64, col[c]], start=True, stop=True).then_inc(s["dps"], 1)
        pe.wait_ge(s["addx"], 3)
        for c in range(2):
            for i in range(4):
                tok = slice((4 * c + i) * P, (4 * c + i + 1) * P)
                o = nc.tensor.matmul(ps[4 + c][:, i * P:(i + 1) * P], mixed[:, 2, tok], W["v"], start=True, stop=True)
            o.then_inc(s["vps"], 1)
        pe.wait_ge(s["addx"], 4)
        for c in range(2):
            nc.tensor.matmul(ps[6 + c][:, :], W["r"], mixed[:, 3, col[c]], start=True, stop=True).then_inc(s["rps"], 1)

        def scores(step, kk, rr):
            h = 1 << (step - 1)
            for bi in range(B * TILES):
                tok = slice(bi * P, (bi + 1) * P)
                o = nc.tensor.matmul(ps[4 * (step % 2) + bi // 4][:, (bi % 4) * P:(bi % 4 + 1) * P], kk[:, tok],
                                     rr[:, :, tok].rearrange("p e (b h m) -> p e b h m", h=2, m=h)[:, :, :, 1, :], start=True, stop=True)
            o.then_inc(s["gps"], 1)

        def diagonal(kk, rr):
            for bi in range(B * TILES):
                tok = slice(bi * P, (bi + 1) * P)
                o = nc.tensor.matmul(ps[bi // 2][:, (bi % 2) * 2 * P:(bi % 2 + 1) * 2 * P], kk[:, tok], rr[:, :, tok], start=True, stop=True)
            o.then_inc(s["gps"], 1)

        pe.wait_ge(s["ku"], 1)
        pe.wait_ge(s["rev"], 4)
        pe.wait_ge(s["wev"], 2)
        diagonal(kp[0], R2)
        pe.wait_ge(s["vev"], 2)
        pe.wait_ge(s["consts"], NCONST)
        scores(1, K, R2)
        for lv in range(1, LEVELS - 1):
            pe.wait_ge(s["kpr"], lv)
            pe.wait_ge(s["rpr"], lv)
            pe.wait_ge(s["gcp"], lv)
            scores(lv + 1, kp[lv % 2], rp[lv % 2])
        lv = LEVELS - 1
        pe.wait_ge(s["kpr"], lv)
        pe.wait_ge(s["rpr"], lv)
        pe.wait_ge(s["gcp"], lv)
        for b in range(B):
            o = nc.tensor.matmul(ps[b // 2][:, (b % 2) * 2 * P:(b % 2 + 1) * 2 * P],
                                 kp[lv % 2][:, b * T:b * T + P], rp[lv % 2][:, :, b * T + P:(b + 1) * T], start=True, stop=True)
        o.then_inc(s["gps"], 1)
        pe.wait_ge(s["xev"], 2)
        pe.wait_ge(s["gcp"], LEVELS)
        for c in range(2):
            for b in (2 * c, 2 * c + 1):
                for h in range(RH):
                    r = slice(h * RD, (h + 1) * RD)
                    o0 = (b % 2) * T
                    vt = lambda i: V[:, (b * TILES + i) * P + h * RD:(b * TILES + i) * P + (h + 1) * RD]
                    st = lambda i: S[:, ((b * TILES + i) * RH + h) * P:((b * TILES + i) * RH + h + 1) * P]
                    nc.tensor.matmul(ps[4 + c][r, o0:o0 + P], vt(0), st(0), start=True, stop=True)
                    nc.tensor.matmul(ps[4 + c][r, o0 + P:o0 + T], vt(0), SX[:, (b * RH + h) * P:(b * RH + h + 1) * P], start=True, stop=False)
                    o = nc.tensor.matmul(ps[4 + c][r, o0 + P:o0 + T], vt(1), st(1), start=False, stop=True)
            o.then_inc(s["yps"], 1)
        for c in range(2):
            pe.wait_ge(s["yev"], c + 1)
            nc.tensor.matmul(ps[c][:, :], g["blk"][:, :], Y[:, col[c]], start=True, stop=True).then_inc(s["mean"], 1)
        for c in range(2):
            pe.wait_ge(s["squared"], c + 1)
            nc.tensor.matmul(ps[2 + c][:, :], g["blk"][:, :], sq[:, col[c]], start=True, stop=True).then_inc(s["var"], 1)
        for c in range(2):
            pe.wait_ge(s["yna"], c + 1)
            nc.tensor.matmul(ps[4 + c][:, :], W["o"], yc[:, col[c]], start=True, stop=True).then_inc(s["ops"], 1)


def cross_attention_inputs(nc, g):
    GROUPS = XH // HG

    def sb(name, shape, dt=F32):
        return g["sb"](f"xa_{name}", shape, dt)

    wts = sb("wts", [P, (4 + GROUPS) * P])
    cw = sb("cw", [CC, 2 * P])
    vec = sb("vec", [P, 5])
    vb = sb("vb", [P, 2, P])
    ctxT = sb("ctxT", [CC, B * P])
    hm = sb("hm", [P, XH])
    causal = sb("causal", [P, HG * P], BF16)
    loads = ((wts[:, :], "xa_w"), (cw[:, :], "xa_cw"), (vec[:, :], "xa_vec"), (vb[:, :, :], "xa_vb"),
             (ctxT[:, :], "ctxT"), (hm[:, :], "xa_hm"), (causal[:, :], "xa_causal"))
    return {"wts": wts, "cw": cw, "vec": vec, "vb": vb, "ctxT": ctxT, "hm": hm, "causal": causal, "loads": loads, "in": g["sem"]("xa_in")}


def cross_attention(nc, g, scope):
    ps, t, sem, X, Z = g["ps"], g["t"], g["sem"], g["X"], g["Z"]
    ident, identb = g["ident"], g["identb"]
    GROUPS = XH // HG
    SCALE = XD ** -0.5

    def sb(name, shape, dt=F32):
        return scope.enter_context(nc.sbuf_tensor(f"xa_{name}", shape, dt))

    xa = g["xa"]
    wts, cw, vec, vb, ctxT, hm, causal = (xa[n] for n in ("wts", "cw", "vec", "vb", "ctxT", "hm", "causal"))
    xb = sb("xb", [P, T])
    cb = sb("cb", [CC, P])
    qT, kT, qcT = (sb(n, [P, T]) for n in ("qT", "kT", "qcT"))
    kcT = sb("kcT", [P, B * CTX])
    kz = [sb(f"kz{i}", [P, HG, T]) for i in range(2)]
    kcz = [sb(f"kcz{i}", [P, HG, CTX]) for i in range(2)]
    V = sb("V", [P, TILES, XH, XPAD])
    Vc = sb("Vc", [P, XH // 2, 2 * XPAD])
    Pb = [sb(f"Pb{i}", [P, 4 * HALF]) for i in range(GROUPS)]
    PT = [sb(f"PT{i}", [P, 2 * HALF]) for i in range(2)]
    mx, sm, rc = (sb(n, [P, GROUPS, 16]) for n in ("mx", "sm", "rc"))
    Y = sb("Y", [P, GROUPS, T])
    Wq, Wk, Wcq = (wts[:, i * P:(i + 1) * P] for i in range(3))
    Wv = wts[:, 3 * P:4 * P]
    Wp = wts[:, 4 * P:].rearrange("p (g c) -> p g c", g=GROUPS)

    BANKS = [(0, 2, T), (2, 4, T), (4, 8, P), (8, 16, CTX)]
    rows = lambda a, n: a.rearrange("p (h k) -> p h k", k=n)
    bank_of = lambda a, i: a[:, i * HALF:(i + 1) * HALF]

    names = ["zero", "xb", "qps", "qcps", "kcps", "kev", "qev", "qcev", "kcev", "kz", "kcz", "vps", "vev",
             "sps", "max", "nmx", "exp", "rc", "pn", "tps", "pev", "pv", "yev", "wps", "res"]
    s = {n: sem(f"xa_{n}") for n in names}
    block = scope.enter_context(nc.Block())

    def run(slot):
        def over(eng):
            for u in range(GROUPS):
                slot(0, u, lambda d: u >= d, False)
            with eng.Fori(1, B) as b:
                for u in range(GROUPS):
                    slot(b, u, lambda d: True, True)
            for u in range(GROUPS):
                slot(B, u, lambda d: u < d, True)
        return over

    @block.sync
    def _(sp):
        la = g["la"]
        sp.dma_start(la["qks"][:, :, :, :], t["la_qks"]).then_inc(la["in"], 16)
        sp.dma_start(la["tc"][:, :, :, :], t["la_tc"]).then_inc(la["in"], 16)
        sp.dma_start(la["mask"][:, :, :], t["la_mask"]).then_inc(la["in"], 16)
        for p in range(PAIRS):
            sp.dma_start(la["Wqkv"][:, p, :], t["la_wqkv"][0, :, p, :]).then_inc(la["wqkv_in"][p], 16)

    NIN = 16 * len(xa["loads"])

    @block.tensor
    def _(pe):
        pe.wait_ge(xa["in"], NIN)
        nc.tensor.matmul(ps[6][:, 0:B * CTX], cw[:, 0:P], ctxT[:, :].rearrange("c (b r k) -> c b r k", b=B, r=2)[:, :, 0, :],
                         start=True, stop=True).then_inc(s["kcps"], 1)
        pe.wait_ge(s["kcev"], 1)

        def queries_keys(b):
            nc.tensor.matmul(ps[7][:, 0:T], Wk, X[:, bass.ds(b * T, T)], start=True, stop=True)
            nc.tensor.matmul(ps[7][:, T:2 * T], Wq, X[:, bass.ds(b * T, T)], start=True, stop=True).then_inc(s["qps"], 1)

        queries_keys(0)

        def slot(b, u, live, tail):
            g = GROUPS * b + u
            qk = lambda i: scores(g, u, i, live)
            if live(0):
                if u == 0:
                    pe.wait_ge(s["xb"], 2 * b + 2)
                    pe.wait_ge(s["qev"], b + 1)
                    for i in range(TILES):
                        nc.tensor.matmul(ps[7][:, i * P:(i + 1) * P], xb[:, i * P:(i + 1) * P], Wv, start=True, stop=True)
                    nc.tensor.matmul(ps[7][:, 2 * P:3 * P], cb[:, :], cw[:, P:2 * P], start=True, stop=True).then_inc(s["vps"], 1)
                pe.wait_ge(s["kz"], g + 1)
                qk(0)
            if live(2):
                turned(g, u, 0)
            if live(0):
                qk(1)
            if tail and u == 3:
                pe.wait_ge(s["yev"], GROUPS * b)
                if live(0):
                    pe.wait_ge(s["vev"], 6 * b + 6)
                for n in range(GROUPS):
                    o = nc.tensor.matmul(ps[7][:, 0:T], Wp[:, n, :], Y[:, n, :], start=(n == 0), stop=(n == GROUPS - 1))
                o.then_inc(s["wps"], 1)
            if live(0):
                qk(2)
                if u == 0:
                    if live(3):
                        pe.wait_ge(s["yev"], g - 2)
                    nc.tensor.matmul(ps[6][:, 0:T], Wcq, X[:, bass.ds(b * T, T)], start=True, stop=True).then_inc(s["qcps"], 1)
            if live(2):
                turned(g, u, 1)
            if live(0) and u == 3:
                if tail:
                    pe.wait_ge(s["res"], b)
                else:
                    pe.wait_ge(s["vev"], 6)
                queries_keys((b + 1) % B)
            if live(0) and u == 0:
                pe.wait_ge(s["qcev"], b + 1)
            if live(2):
                weighted(b, g, u, 0, live)
            if live(0):
                qk(3)
            if live(2):
                weighted(b, g, u, 1, live)

        def scores(g, u, i, live):
            if live(1):
                pe.wait_ge(s["exp"], 4 * (g - 1) + i + 1)
            if i == 3:
                pe.wait_ge(s["kcz"], g + 1)
            kk, kc = kz[u % 2], kcz[u % 2]
            if i < 2:
                nc.tensor.matmul(ps[i][:, :], qT[:, P:T], kk[:, 2 * i:2 * i + 2, :], start=True, stop=False, skip_group_check=True)
                nc.tensor.matmul(rows(ps[i][:, :], T)[:, :, P:T], identb[:, :], causal[:, 0:2 * P], start=False, stop=True,
                                 skip_group_check=True).then_inc(s["sps"], 1)
            elif i == 2:
                nc.tensor.matmul(ps[2][:, :], qT[:, 0:P], kk[:, :, 0:P], start=True, stop=False)
                nc.tensor.matmul(ps[2][:, :], identb[:, :], causal[:, :], start=False, stop=True).then_inc(s["sps"], 1)
            else:
                for q in range(TILES):
                    o = nc.tensor.matmul(ps[3][:, q * T:(q + 1) * T], qcT[:, q * P:(q + 1) * P], kc[:, :, :], start=True, stop=True)
                o.then_inc(s["sps"], 1)

        def turned(g, u, i):
            p = Pb[(u - 2) % GROUPS]
            n = g - 2
            pe.wait_ge(s["pn"], 4 * n + 4)
            if i:
                pe.wait_ge(s["pev"], 2 * (2 * n + 1))
            for h in range(2):
                hh = 2 * i + h
                q1 = hh * T
                q0 = 2 * HALF + hh * P
                nc.tensor.transpose(ps[4][:, h * T:h * T + P], p[:, q0:q0 + P], ident[:, :])
                nc.tensor.transpose(ps[4][:, h * T + P:(h + 1) * T], p[:, q1:q1 + P], ident[:, :])
                nc.tensor.transpose(ps[5][:, h * P:(h + 1) * P], p[:, q1 + P:q1 + T], ident[:, :])
            for q in range(TILES):
                c0 = 3 * HALF + q * T + i * P
                o = nc.tensor.transpose(ps[5][:, T + q * P:T + (q + 1) * P], p[:, c0:c0 + P], ident[:, :])
            o.then_inc(s["tps"], 1)

        def weighted(b, g, u, i, live):
            n = g - 2
            un = (u - 2) % GROUPS
            pe.wait_ge(s["pev"], 2 * (2 * n + i + 1))
            if i == 0:
                pe.wait_ge(s["vev"], 6 * b + (3 if u >= 2 else 0))
                if live(3):
                    pe.wait_ge(s["yev"], n)
            pt = PT[i]
            for h in range(2):
                hh = 2 * i + h
                v = slice(hh * XPAD, (hh + 1) * XPAD)
                nc.tensor.matmul(ps[6][v, 0:T], V[:, 0, HG * un + hh, :], pt[:, h * T:(h + 1) * T], start=True, stop=False, skip_group_check=True)
                nc.tensor.matmul(ps[6][v, P:T], V[:, 1, HG * un + hh, :], pt[:, HALF + h * P:HALF + (h + 1) * P], start=False, stop=False, skip_group_check=True)
            nc.tensor.matmul(ps[6][64 * i:64 * i + 64, 0:T], Vc[:, 2 * un + i, :], pt[:, HALF + T:], start=False, stop=True,
                             skip_group_check=True).then_inc(s["pv"], 1)

        run(slot)(pe)

    @block.vector
    def _(dve):
        nc.vector.memset(Vc[:, :, :], 0.0).then_inc(s["zero"], 1)
        nc.vector.memset(V[:, :, :, :], 0.0).then_inc(s["zero"], 1)
        dve.wait_ge(xa["in"], NIN)
        dve.wait_ge(s["zero"], 2)
        dve.wait_ge(s["kcev"], 1)

        def batch_in(b):
            nc.vector.tensor_scalar(xb[:, :], X[:, bass.ds(b * T, T)], 1.0, None, ALU.mult).then_inc(s["xb"], 1)
            nc.vector.tensor_scalar(cb[:, :], ctxT[:, bass.ds(b * P, P)], 1.0, None, ALU.mult).then_inc(s["xb"], 1)

        def slot(b, u, live, tail):
            g = GROUPS * b + u
            if live(0):
                maxima(g, u, 0)
            if live(2):
                turned(g, 0, live)
            if live(1):
                dve.wait_ge(s["exp"], 4 * g)
                nc.vector.reciprocal(rc[:, (u - 1) % GROUPS, :], sm[:, (u - 1) % GROUPS, :]).then_inc(s["rc"], 1)
            if live(0):
                maxima(g, u, 1)
                maxima(g, u, 2)
            if tail and u == 3:
                o = (b - 1) * T
                dve.wait_ge(s["wps"], b)
                nc.vector.scalar_tensor_tensor(Z[:, bass.ds(o, T)], ps[7][:, 0:T], vec[:, 4:5], X[:, bass.ds(o, T)],
                                               ALU.add, ALU.add).then_inc(s["res"], 1)
            if live(2):
                turned(g, 1, live)
            if live(0):
                if u in (0, 2):
                    values(b, u)
                if u < 3:
                    context_keys(b, u + 1)
                else:
                    batch_in((b + 1) % B)
                    context_keys((b + 1) % B, 0)
                maxima(g, u, 3)

        def values(b, u):
            if u == 0:
                dve.wait_ge(s["vps"], b + 1)
            hs = slice(HG * u, HG * u + 2 * HG)
            nc.vector.tensor_tensor(V[:, :, hs, 0:XD], ps[7][:, 0:2 * P].rearrange("p (t h d) -> p t h d", t=TILES, d=XD)[:, :, hs, :],
                                    vb[:, 0:1, :].rearrange("p o (h d) -> p o h d", d=XD)[:, :, hs, :].broadcast_to([P, TILES, 2 * HG, XD]),
                                    ALU.add).then_inc(s["vev"], 1)
            for h in range(2):
                r = slice(64 * h, 64 * h + 64)
                pairs = slice(HG * u // 2, HG * u // 2 + HG)
                half = lambda a: a.rearrange("p (n h d) -> p n h d", h=2, d=XD)[:, pairs, h, :]
                nc.vector.tensor_tensor(Vc[r, pairs, h * XPAD:h * XPAD + XD], half(ps[7][r, 2 * P:3 * P]), half(vb[r, 1, :]),
                                        ALU.add).then_inc(s["vev"], 1)

        def context_keys(b, u):
            nc.vector.tensor_tensor(kcz[u % 2][:, :, :], kcT[:, bass.ds(b * CTX, CTX)].rearrange("p (o k) -> p o k", o=1).broadcast_to([P, HG, CTX]),
                                    hm[:, HG * u:HG * u + HG].rearrange("p (h o) -> p h o", o=1).broadcast_to([P, HG, CTX]),
                                    ALU.mult).then_inc(s["kcz"], 1)

        def maxima(g, u, i):
            lo, hi, n = BANKS[i]
            dve.wait_ge(s["sps"], 4 * g + i + 1)
            nc.vector.tensor_reduce(mx[:, u, lo:hi], rows(ps[i][:, :], n), AX_X, ALU.max).then_inc(s["max"], 1)
            dve.wait_ge(s["max"], 4 * g + i + 1)
            nc.vector.tensor_scalar(mx[:, u, lo:hi], mx[:, u, lo:hi], -SCALE, None, ALU.mult).then_inc(s["nmx"], 1)

        def turned(g, i, live):
            n = g - 2
            dve.wait_ge(s["tps"], 2 * n + i + 1)
            if live(3):
                dve.wait_ge(s["pv"], 2 * (n - 1) + i + 1)
            for c in range(2):
                nc.vector.tensor_copy(PT[i][:, c * HALF:(c + 1) * HALF], ps[4 + c][:, :]).then_inc(s["pev"], 1)

        batch_in(0)
        context_keys(0, 0)
        run(slot)(dve)

    @block.gpsimd
    def _(pool):
        shared = g
        clear_buffers(nc, g)
        rotary_tables(nc, g, pool, range(2))

        def slot(b, u, live, tail):
            if live(1):
                g = GROUPS * b + u
                un = (u - 1) % GROUPS
                pool.wait_ge(s["rc"], g)
                for i, (lo, hi, n) in enumerate(BANKS):
                    a = rows(bank_of(Pb[un], i), n)
                    r = rc[:, un, lo:hi].rearrange("p (h o) -> p h o", o=1).broadcast_to([P, hi - lo, n])
                    nc.gpsimd.tensor_tensor(a, a, r, ALU.mult).then_inc(s["pn"], 1)
            if live(1) and not tail:
                rotary_tables(nc, shared, pool, (u + 1,))

        run(slot)(pool)
        rotary_tables(nc, shared, pool, range(GROUPS + 1, DEPTH))

    @block.scalar
    def _(act):
        act.wait_ge(xa["in"], NIN)
        act.wait_ge(s["kcps"], 1)
        nc.scalar.activation(kcT[:, :], ps[6][:, 0:B * CTX], ACT.Identity, bias=vec[:, 3:4]).then_inc(s["kcev"], 1)

        def slot(b, u, live, tail):
            g = GROUPS * b + u
            if live(0):
                if tail:
                    act.wait_ge(s["tps"], 2 * (g - 3))
                exps(g, u, 0)
            if live(3):
                act.wait_ge(s["pv"], 2 * (g - 2))
                if tail and u == 3:
                    act.wait_ge(s["wps"], b)
                nc.scalar.copy(Y[:, (u - 3) % GROUPS, :], ps[6][:, 0:T]).then_inc(s["yev"], 1)
            if live(0):
                exps(g, u, 1)
                if u == 0:
                    act.wait_ge(s["qcps"], b + 1)
                    nc.scalar.activation(qcT[:, :], ps[6][:, 0:T], ACT.Identity, bias=vec[:, 2:3]).then_inc(s["qcev"], 1)
                if u < 3:
                    keys(g + 1, u + 1, live)
                exps(g, u, 2)
                if u == 3:
                    queries_keys(b + 1)
                    keys(g + 1, 0, live)
                exps(g, u, 3)

        def keys(g, u, live):
            if u == 0:
                act.wait_ge(s["kev"], g // GROUPS + 1)
            if live(1):
                act.wait_ge(s["sps"], 4 * (g - 1))
            for h in range(HG):
                o = nc.scalar.activation(kz[u % 2][:, h, :], kT[:, :], ACT.Copy, scale=hm[:, HG * u + h:HG * u + h + 1])
            o.then_inc(s["kz"], 1)

        def queries_keys(b):
            act.wait_ge(s["qps"], b + 1)
            nc.scalar.activation(kT[:, :], ps[7][:, 0:T], ACT.Identity, bias=vec[:, 1:2]).then_inc(s["kev"], 1)
            nc.scalar.activation(qT[:, :], ps[7][:, T:2 * T], ACT.Identity, bias=vec[:, 0:1]).then_inc(s["qev"], 1)

        def exps(g, u, i):
            lo, hi, n = BANKS[i]
            act.wait_ge(s["nmx"], 4 * g + i + 1)
            for r in range(hi - lo):
                o = nc.scalar.activation(Pb[u][:, i * HALF + r * n:i * HALF + (r + 1) * n], ps[i][:, r * n:(r + 1) * n], ACT.Exp,
                                         scale=SCALE, bias=mx[:, u, lo + r:lo + r + 1], accum_out=sm[:, u, lo + r:lo + r + 1])
            o.then_inc(s["exp"], 1)

        queries_keys(0)
        keys(0, 0, lambda d: False)
        run(slot)(act)


def local_layers_inputs(nc, g):
    def sb(name, shape, dt=F32):
        return g["sb"](f"la_{name}", shape, dt)

    Wqkv = sb("Wqkv", [P, PAIRS, 3 * P])
    qks = sb("qks", [P, DEPTH, 2, 2 * LD])
    tc = sb("tc", [P, 2, TILES, 2 * P])
    tab = sb("tab", [P, DEPTH * 2 * HALF])
    mask = sb("mask", [P, TILES, 2 * SEG], BF16)
    kz = [sb(f"kz{i}", [P, 2, T]) for i in range(2)]
    PW = [sb(f"PW{i}", [P, 2, WIN]) for i in range(2)]
    av, gt = sb("av", [P, len(FC), T]), sb("gt", [P, len(FC), T])
    pr = [sb(f"pr{i}", [P, P - WIN + TILES * 2 * SEG]) for i in range(2)]
    return {"pr": pr, "Wqkv": Wqkv, "qks": qks, "tc": tc, "tab": tab, "mask": mask, "kz": kz, "PW": PW, "av": av, "gt": gt,
            "in": g["sem"]("la_in"), "zero": g["sem"]("la_zero"), "tabs": g["sem"]("la_tabs"),
            "wqkv_in": [g["sem"](f"la_wqkv_in{p}") for p in range(PAIRS)]}


def clear_buffers(nc, g):
    la = g["la"]
    for a in (*la["kz"], *la["PW"], la["gt"], la["av"], *la["pr"]):
        nc.gpsimd.memset(a[:], 0.0).then_inc(la["zero"], 1)


def rotary_tables(nc, g, pool, layers):
    la = g["la"]
    pool.wait_ge(la["in"], 48)
    for layer in layers:
        for i in range(2):
            for q in range(2):
                part = lambda a: a.rearrange("p (t q c) -> p t q c", t=TILES, q=2)[:, :, q, :]
                table = la["tab"][:, (2 * layer + i) * HALF:(2 * layer + i + 1) * HALF]
                nc.gpsimd.tensor_tensor(part(table), part(la["tc"][:, i, :, :].rearrange("p t c -> p (t c)")),
                                        la["qks"][:, layer, q:q + 1, :].broadcast_to([P, TILES, 2 * LD]), ALU.mult).then_inc(la["tabs"], 1)


def local_layers(nc, g, scope):
    ps, t, sem, X, X0 = g["ps"], g["t"], g["sem"], g["Z"], g["X"]
    ident, eps = g["ident"], g["eps"]
    STEPS = DEPTH * B

    def sb(name, shape, dt=F32):
        return scope.enter_context(nc.sbuf_tensor(f"la_{name}", shape, dt))

    la = g["la"]
    Wqkv, tab, mask, kz, PW, av, gt = (la[n] for n in ("Wqkv", "tab", "mask", "kz", "PW", "av", "gt"))
    pr = la["pr"]
    Wo = sb("Wo", [P, PAIRS, P])
    W1 = sb("W1", [P, 2 * INNER])
    W2 = sb("W2", [P, len(FC), P])
    vec = sb("vec", [P, 8])
    b2 = sb("b2", [P, 1])
    xs = sb("xs", [P, T])
    V = sb("V", [P, PAIRS, TILES, P])
    t1, t2, sq, qk = ([sb(f"{n}{i}", [P, HALF]) for i in range(2)] for n in ("t1", "t2", "sq", "qk"))
    ss, rn = ([sb(f"{n}{i}", [P, 8]) for i in range(2)] for n in ("ss", "rn"))
    qT = [sb(f"qT{i}", [P, T]) for i in range(2)]
    mx, sm, rc = ([sb(f"{n}{i}", [P, 4]) for i in range(2)] for n in ("mx", "sm", "rc"))
    PT = [sb(f"PT{i}", [P, 2, T]) for i in range(2)]
    OT = sb("OT", [P, PAIRS, T])
    xf, xc, sqf = sb("xf", [P, T]), sb("xc", [P, T]), sb("sqf", [P, T])

    per_pair = ["proj", "t1", "t2", "ss", "ssg", "sq", "vev", "ln", "rn", "rot", "qk", "tr", "tev", "sc", "max", "exp",
                "rc", "pn", "pt", "pw", "ptev", "pwev", "pv", "otev"]
    per_step = ["xs", "wo", "x1", "xf", "mean", "xc", "sqf", "var", "lnv", "rstd", "xn", "xng", "hg", "av", "gb", "gelu", "hs", "w2", "x2"]
    s = {n: sem(f"la_{n}") for n in per_pair + per_step + ["x0", "wo_in", "w1_in", "w2_in"]}
    block = scope.enter_context(nc.Block())
    banks = g["psum"][:, 0:TILES * HALF].rearrange("p (t c) -> p t c", t=TILES)
    qk_banks, v_banks = banks[:, :, 0:2 * P], banks[:, :, 2 * P:3 * P]
    row = lambda i, h: P - WIN + (2 * (1 - i) + h) * SEG
    heads = lambda a: a.rearrange("p (h d) -> p h d", d=LD)
    seg = lambda a: a.rearrange("p (h k) -> p h k", k=SEG)
    bc = lambda a, n: a.rearrange("p (h o) -> p h o", o=1).broadcast_to([P, a.shape[1], n])

    def run(eng, slot):
        for j in range(2):
            for p in range(PAIRS):
                slot(j, p, lambda d: PAIRS * j + p >= d, j >= 1, False)
        with eng.Fori(2, STEPS) as j:
            for p in range(PAIRS):
                slot(j, p, lambda d: True, True, True)
        for p in range(PAIRS):
            slot(STEPS, p, lambda d: p < d, True, True)
        for p in range(PAIRS):
            slot(STEPS + 1, p, lambda d: False, False, True)

    @block.sync
    def _(sp):
        def load(layer, later):
            if later:
                for p in range(PAIRS):
                    sp.wait_ge(s["proj"], PAIRS * (B * layer - 1) + p + 1)
                    sp.dma_start(Wqkv[:, p, :], t["la_wqkv"][layer, :, p, :]).then_inc(la["wqkv_in"][p], 16)
                sp.wait_ge(s["wo"], B * layer)
            sp.dma_start(Wo[:, :, :], t["la_wo"][layer]).then_inc(s["wo_in"], 16)
            if later:
                sp.wait_ge(s["gb"], 3 * B * layer)
            sp.dma_start(W1[:, :], t["la_w1"][layer]).then_inc(s["w1_in"], 16)
            sp.dma_start(vec[:, :], t["la_vec"][layer]).then_inc(s["w1_in"], 16)
            if later:
                sp.wait_ge(s["x2"], B * layer)
            sp.dma_start(W2[:, :, :], t["la_w2"][layer]).then_inc(s["w2_in"], 16)
            sp.dma_start(b2[:, :], t["la_b2"][layer]).then_inc(s["w2_in"], 16)

        load(0, False)
        with sp.Fori(1, DEPTH) as layer:
            load(layer, True)

    @block.tensor
    def _(pe):
        pe.wait_ge(la["in"], 48)
        pe.wait_ge(la["zero"], 8)

        def slot(j, p, live, front, back):
            k = PAIRS * j + p
            if live(0):
                if p == 0:
                    pe.wait_ge(s["xs"], 2 * j + 2)
                pe.wait_ge(la["wqkv_in"][p], 16 * (j // B) + 16)
            if live(5):
                pe.wait_ge(s["pwev"], k - 4)
            elif live(1):
                pe.wait_ge(s["vev"], k)
            if live(4):
                pe.wait_ge(s["pn"], 2 * (k - 3) - 1)
            if live(0):
                nc.tensor.matmul(ps[0][:, 0:3 * P], xs[:, 0:P], Wqkv[:, p, :], start=True, stop=True)
            if live(4):
                for h in range(2):
                    c1 = row(1, h) + WIN
                    o = nc.tensor.transpose(ps[1][:, 3 * P + h * WIN:3 * P + (h + 1) * WIN], pr[p % 2][0:WIN, c1 - P:c1], ident[0:WIN, 0:WIN])
                o.then_inc(s["pw"], 1)
            if live(0):
                nc.tensor.matmul(ps[1][:, 0:3 * P], xs[:, P:2 * P], Wqkv[:, p, :], start=True, stop=True).then_inc(s["proj"], 1)
            if front and p == 5:
                pe.wait_ge(s["wo_in"], 16 * ((j - 1) // B) + 16)
                pe.wait_ge(s["otev"], PAIRS * j)
                if back:
                    pe.wait_ge(s["gb"], 3 * (j - 1))
                for q in range(PAIRS):
                    o = nc.tensor.matmul(ps[6][:, 0:T], Wo[:, q, :], OT[:, q, :], start=(q == 0), stop=(q == PAIRS - 1))
                o.then_inc(s["wo"], 1)
            if front and p == 6:
                pe.wait_ge(s["xf"], 2 * j)
                nc.tensor.matmul(ps[6][:, 0:T], g["ones"][:, :], xf[:, :], start=True, stop=True).then_inc(s["mean"], 1)
            if live(4):
                if live(5):
                    pe.wait_ge(s["ptev"], k - 4)
                pe.wait_ge(s["pn"], 2 * (k - 3))
                for h in range(2):
                    for i in range(TILES):
                        c0 = row(i, h) + WIN
                        o = nc.tensor.transpose(ps[5][:, h * T + i * P:h * T + (i + 1) * P], pr[p % 2][:, c0:c0 + P], ident[:, :])
                o.then_inc(s["pt"], 1)
            if live(2):
                pe.wait_ge(s["tev"], 3 * (k - 1))
                if live(3):
                    pe.wait_ge(s["max"], k - 2)
                qq, kk = qT[p % 2], kz[p % 2]
                nc.tensor.matmul(seg(ps[3][:, 0:2 * SEG])[:, :, WIN:], qq[:, 0:P], kk[:, :, 0:P], start=True, stop=True)
                nc.tensor.matmul(seg(ps[4][:, 0:2 * SEG]), qq[:, P:T], kk[:, :, P - WIN:T], start=True, stop=True).then_inc(s["sc"], 1)
            if live(5):
                if not live(4):
                    pe.wait_ge(s["ptev"], k - 4)
                if live(6):
                    pe.wait_ge(s["otev"], k - 5)
                v = V[:, (p - 5) % PAIRS, :, :]
                for h in range(2):
                    r = slice(h * LD, (h + 1) * LD)
                    pt = PT[(p + 1) % 2]
                    nc.tensor.matmul(ps[7][r, 0:P], v[:, 0, r], pt[:, h, 0:P], start=True, stop=True)
                    nc.tensor.matmul(ps[7][r, P:T], v[:, 1, r], pt[:, h, P:T], start=True, stop=False, skip_group_check=True)
                    o = nc.tensor.matmul(ps[7][r, P:P + WIN], v[:, 0, r], PW[(p + 1) % 2][:, h, :], start=False, stop=True, skip_group_check=True)
                o.then_inc(s["pv"], 1)
            if live(1):
                pe.wait_ge(s["qk"], k)
                q = qk[(p + 1) % 2]
                for i in range(TILES):
                    nc.tensor.transpose(ps[2][:, i * P:(i + 1) * P], q[:, 2 * P * i:2 * P * i + P], ident[:, :])
                    o = nc.tensor.transpose(ps[2][:, T + i * P:T + (i + 1) * P], q[:, 2 * P * i + P:2 * P * (i + 1)], ident[:, :])
                o.then_inc(s["tr"], 1)
            if back and p == 6:
                if front:
                    pe.wait_ge(s["xc"], j)
                pe.wait_ge(s["w2_in"], 32 * ((j - 2) // B) + 32)
                pe.wait_ge(s["hs"], j - 1)
                for c, (_, n) in enumerate(FC):
                    o = nc.tensor.matmul(ps[6][:, 0:T], W2[0:n, c, :], av[0:n, c, :], start=(c == 0), stop=(c == len(FC) - 1))
                o.then_inc(s["w2"], 1)
            if front and p == 7:
                pe.wait_ge(s["sqf"], j)
                if back:
                    pe.wait_ge(s["x2"], j - 1)
                nc.tensor.matmul(ps[6][:, 0:T], g["ones"][:, :], sqf[:, :], start=True, stop=True).then_inc(s["var"], 1)
            if back and 1 <= p <= 3:
                hidden(j - 1, p - 1)

        def hidden(i, c):
            f0, n = FC[c]
            if c == 0:
                pe.wait_ge(s["w1_in"], 32 * ((i - 1) // B) + 32)
                pe.wait_ge(s["xng"], i)
            else:
                pe.wait_ge(s["gb"], 3 * (i - 1) + c)
            nc.tensor.matmul(ps[6][0:n, 0:T], W1[:, f0:f0 + n], xc[:, :], start=True, stop=True)
            nc.tensor.matmul(ps[6][0:n, T:2 * T], W1[:, INNER + f0:INNER + f0 + n], xc[:, :], start=True, stop=True).then_inc(s["hg"], 1)

        run(pe, slot)

    @block.vector
    def _(dve):
        nc.vector.tensor_copy(X[:, :], X0[:, :]).then_inc(s["x0"], 1)
        dve.wait_ge(s["x0"], 1)
        dve.wait_ge(la["zero"], 8)
        dve.wait_ge(la["tabs"], 4 * DEPTH)

        def shift_in(dst, src, off, done):
            nc.vector.tensor_scalar(dst[0:64, :], src[0:64, bass.ds(off, T)], 1.0, None, ALU.mult).then_inc(done, 1)
            nc.vector.tensor_scalar(dst[64:P, 1:T], src[64:P, bass.ds(off, T - 1)], 1.0, None, ALU.mult).then_inc(done, 1)

        nc.vector.memset(xs[64:P, 0:1], 0.0)
        nc.vector.memset(xf[64:P, 0:1], 0.0)
        shift_in(xs, X, 0, s["xs"])

        def slot(j, p, live, front, back):
            k = PAIRS * j + p
            a = p % 2
            off1 = ((j - 1) % B) * T if front else None
            off2 = ((j - 2) % B) * T if back else None
            if back and p == 7:
                dve.wait_ge(s["w2"], j - 1)
                nc.vector.scalar_tensor_tensor(X[:, bass.ds(off2, T)], ps[6][:, 0:T], b2[:, 0:1], X[:, bass.ds(off2, T)],
                                               ALU.add, ALU.add).then_inc(s["x2"], 1)
            if back and p == 1:
                dve.wait_ge(s["rstd"], j - 1)
                nc.vector.tensor_tensor(xc[:, :], xc[:, :], sqf[:, :], ALU.mult).then_inc(s["xn"], 1)
                dve.wait_ge(s["xn"], j - 1)
                dve.wait_ge(s["w1_in"], 32 * ((j - 2) // B) + 32)
                nc.vector.tensor_scalar(xc[:, :], xc[:, :], vec[:, 6:7], vec[:, 7:8], ALU.mult, ALU.add).then_inc(s["xng"], 1)
            if back and 2 <= p <= 4:
                values(j - 1, p - 2)
            if live(0):
                dve.wait_ge(s["proj"], k + 1)
                if live(2):
                    dve.wait_ge(s["qk"], k - 1)
                tiles = lambda x: x.rearrange("p (t c) -> p t c", t=TILES)
                nc.vector.tensor_tensor(tiles(t1[a][:, :]), qk_banks, tiles(tab[:, bass.ds(j // B * 2 * HALF, HALF)]), ALU.mult).then_inc(s["t1"], 1)
                nc.vector.tensor_tensor(tiles(t2[a][:, :]), qk_banks, tiles(tab[:, bass.ds(j // B * 2 * HALF + HALF, HALF)]), ALU.mult).then_inc(s["t2"], 1)
            if live(3):
                b = (p + 1) % 2
                dve.wait_ge(s["exp"], k - 2)
                nc.vector.reciprocal(rc[b][:, :], sm[b][:, :]).then_inc(s["rc"], 1)
            if front and p == 5:
                dve.wait_ge(s["wo"], j)
                nc.vector.tensor_tensor(X[:, bass.ds(off1, T)], X[:, bass.ds(off1, T)], ps[6][:, 0:T], ALU.add).then_inc(s["x1"], 1)
                dve.wait_ge(s["x1"], j)
                if back:
                    dve.wait_ge(s["xc"], j - 1)
                shift_in(xf, X, off1, s["xf"])
            if front and p == 6:
                dve.wait_ge(s["mean"], j)
                nc.vector.tensor_tensor(xc[:, :], xf[:, :], ps[6][:, 0:T], ALU.subtract).then_inc(s["xc"], 1)
            if live(4):
                dve.wait_ge(s["pt"], k - 3)
                nc.vector.tensor_copy(PT[a][:, :, :].rearrange("p h t -> p (h t)"), ps[5][:, :]).then_inc(s["ptev"], 1)
            if live(0):
                dve.wait_ge(s["sq"], k + 1)
                nc.vector.tensor_reduce(ss[a][:, :], heads(sq[a][:, :]), AX_X, ALU.add).then_inc(s["ss"], 1)
                dve.wait_ge(s["ss"], k + 1)
                if live(2):
                    dve.wait_ge(s["sc"], k - 1)
                nc.vector.tensor_scalar(ss[a][:, :], ss[a][:, :], 1e-24, None, ALU.max).then_inc(s["ssg"], 1)
            if live(2):
                if not live(0):
                    dve.wait_ge(s["sc"], k - 1)
                for i in range(TILES):
                    for h in range(2):
                        n = 2 * i + h
                        c = slice(h * SEG + (0 if i else WIN), (h + 1) * SEG)
                        dst = pr[a][:, row(i, h) + c.start - h * SEG:row(i, h) + SEG]
                        o = nc.vector.tensor_tensor_reduce(out=dst, in0=ps[3 + i][:, c], in1=mask[:, i, c],
                                                           scale=-QK_SCALE, scalar=BIG, op0=ALU.add, op1=ALU.min, accum_out=mx[a][:, n:n + 1])
                o.then_inc(s["max"], 1)

        def values(i, c):
            n = FC[c][1]
            dve.wait_ge(s["hg"], 3 * (i - 1) + c + 1)
            nc.vector.tensor_scalar(av[0:n, c, :], ps[6][0:n, 0:T], vec[0:n, c:c + 1], None, ALU.add).then_inc(s["av"], 1)

        run(dve, slot)
        dve.wait_ge(s["x2"], STEPS)
        nc.vector.tensor_tensor(X[:, :], X[:, :], X0[:, :], ALU.add)

    @block.gpsimd
    def _(pool):
        def slot(j, p, live, front, back):
            k = PAIRS * j + p
            a = p % 2
            if live(3):
                b = (p + 1) % 2
                pool.wait_ge(s["rc"], k - 2)
                for i in (1, 0):
                    a2 = seg(pr[b][:, row(i, 0):row(i, 0) + 2 * SEG])
                    nc.gpsimd.tensor_tensor(a2, a2, bc(rc[b][:, 2 * i:2 * i + 2], SEG), ALU.mult).then_inc(s["pn"], 1)
            if live(0):
                pool.wait_ge(s["t2"], k + 1)
                half = lambda x: x[:, :].rearrange("p (h u d) -> p h u d", u=2, d=LD // 2)
                nc.gpsimd.tensor_tensor(half(t1[a]), half(t1[a]), half(t2[a])[:, :, ::-1, :], ALU.add).then_inc(s["rot"], 1)
                pool.wait_ge(s["rot"], k + 1)
                pool.wait_ge(s["rn"], k + 1)
                nc.gpsimd.tensor_tensor(heads(qk[a][:, :]), heads(t1[a][:, :]), bc(rn[a][:, :], LD), ALU.mult).then_inc(s["qk"], 1)
            if back and p == 5:
                pool.wait_ge(s["gelu"], j - 1)
                nc.gpsimd.tensor_tensor(av[:, :, :], av[:, :, :], gt[:, :, :], ALU.mult).then_inc(s["hs"], 1)

        run(pool, slot)

    @block.scalar
    def _(act):
        act.wait_ge(la["zero"], 8)

        def slot(j, p, live, front, back):
            k = PAIRS * j + p
            a = p % 2
            if live(2):
                act.wait_ge(s["tr"], k - 1)
                nc.scalar.copy(qT[a][:, :], ps[2][:, 0:T]).then_inc(s["tev"], 1)
                for h in range(2):
                    r = slice(h * LD, (h + 1) * LD)
                    nc.scalar.copy(kz[a][r, h, :], ps[2][r, T:]).then_inc(s["tev"], 1)
            if live(3):
                b = (p + 1) % 2
                act.wait_ge(s["max"], k - 2)
                for i in range(TILES):
                    for h in range(2):
                        n = 2 * i + h
                        c = slice(row(i, h) + (0 if i else WIN), row(i, h) + SEG)
                        o = nc.scalar.activation(pr[b][:, c], pr[b][:, c], ACT.Exp, scale=-1.0, bias=mx[b][:, n:n + 1], accum_out=sm[b][:, n:n + 1])
                o.then_inc(s["exp"], 1)
            if back and 2 <= p <= 4:
                gates(j - 1, p - 2)
            if back and p == 5:
                act.wait_ge(s["gb"], 3 * (j - 1))
                nc.scalar.activation(gt[:, :, :], gt[:, :, :], ACT.Gelu).then_inc(s["gelu"], 1)
                nc.scalar.preload_act_table_set(LN_EXP)
            if live(0) and p == PAIRS - 1:
                off = ((j + 1) % B) * T
                act.wait_ge(s["proj"], k + 1)
                nc.scalar.copy(xs[0:64, :], X[0:64, bass.ds(off, T)]).then_inc(s["xs"], 1)
                nc.scalar.copy(xs[64:P, 1:T], X[64:P, bass.ds(off, T - 1)]).then_inc(s["xs"], 1)
            if live(0):
                act.wait_ge(s["t2"], k + 1)
                nc.scalar.activation(sq[a][:, :].rearrange("p (t c) -> p t c", t=TILES), qk_banks, ACT.Square).then_inc(s["sq"], 1)
                nc.scalar.copy(V[:, p, :, :], v_banks).then_inc(s["vev"], 1)
            if live(4):
                if not live(0):
                    act.wait_ge(s["pw"], k - 3)
                nc.scalar.copy(PW[a][96:P, :, :], ps[1][96:P, 3 * P:3 * P + 2 * WIN].rearrange("p (h q) -> p h q", h=2)).then_inc(s["pwev"], 1)
            if front and p == 6:
                act.wait_ge(s["xc"], j)
                nc.scalar.activation(sqf[:, :], xc[:, :], ACT.Square).then_inc(s["sqf"], 1)
            if live(5):
                act.wait_ge(s["pv"], k - 4)
                if front and p == 5:
                    act.wait_ge(s["wo"], j)
                nc.scalar.copy(OT[:, (p - 5) % PAIRS, :], ps[7][:, 0:T]).then_inc(s["otev"], 1)
            if back and p == 0:
                act.wait_ge(s["var"], j - 1)
                nc.scalar.activation(sqf[:, :], ps[6][:, 0:T], ACT.Ln, bias=eps[:, 0:1]).then_inc(s["lnv"], 1)
                act.wait_ge(s["lnv"], j - 1)
                nc.scalar.activation(sqf[:, :], sqf[:, :], ACT.Exp, scale=-0.5).then_inc(s["rstd"], 1)
            if live(0):
                act.wait_ge(s["ssg"], k + 1)
                nc.scalar.activation(rn[a][:, :], ss[a][:, :], ACT.Ln, scale=SS_SCALE).then_inc(s["ln"], 1)
                act.wait_ge(s["ln"], k + 1)
                nc.scalar.activation(rn[a][:, :], rn[a][:, :], ACT.Exp, scale=-0.5, bias=eps[:, 2:3]).then_inc(s["rn"], 1)

        def gates(i, c):
            n = FC[c][1]
            act.wait_ge(s["av"], 3 * (i - 1) + c + 1)
            nc.scalar.activation(gt[0:n, c, :], ps[6][0:n, T:2 * T], ACT.Identity, bias=vec[0:n, 3 + c:4 + c]).then_inc(s["gb"], 1)

        run(act, slot)


def _constants():
    import numpy as np

    bf16 = lambda a: (np.ascontiguousarray(a, np.float32).view(np.uint32) >> 16).astype(np.uint16)
    i = np.arange(P)
    c = {"ident": np.eye(P, dtype=np.float32), "identb": bf16(np.eye(P)),
         "ones": np.full((P, P), 1.0 / P, np.float32),
         "blk": np.where(i[:, None] // RD == i[None, :] // RD, 1.0 / RD, 0.0).astype(np.float32)}
    eps = np.zeros((P, 4), np.float32)
    eps[:, 0], eps[:, 1], eps[:, 2] = LN_EPS, GN_EPS, 0.5 * np.log(SS_SCALE)
    c["eps"] = eps
    m = np.zeros((P, LEVELS, P), np.int32)
    src, tgt = i[:, None], i[None, :]
    m[:, 0] = src == tgt
    for lv in range(LEVELS - 1):
        h = 1 << lv
        m[:, lv + 1] = (src // (2 * h) == tgt // (2 * h)) & (src % (2 * h) < h) & (tgt % (2 * h) >= h)
    c["tm_masks"] = m
    c["xa_hm"] = (i[:, None] // XD == np.arange(XH)[None, :]).astype(np.float32)
    cut = np.where(i[None, :] > i[:, None], -BIG, 0.0)
    c["xa_causal"] = bf16(np.tile(cut, (1, HG)))
    q, k = i[:, None], np.arange(SEG)[None, :] - WIN
    near = (k <= q) & (q - k <= WIN)
    mask = np.zeros((P, TILES, 2, SEG))
    for tile in range(TILES):
        mask[:, tile] = np.where(near & (k + tile * P >= 0), 0.0, -BIG)[:, None, :]
    c["la_mask"] = bf16(mask.reshape(P, TILES, 2 * SEG))
    half = np.arange(0, LD, 2, dtype=np.float64)
    pos = np.arange(T, dtype=np.float64)
    freqs = (pos[:, None] * (1.0 / 10000.0 ** (half / LD))[None, :])
    scale = ((half + 0.4 * LD) / (1.4 * LD))[None, :] ** ((pos - T // 2) / (WIN // 2))[:, None]
    tc = np.zeros((2, T, 2, 2, 2, LD // 2))
    for n, sc in enumerate((scale, 1.0 / scale)):
        tc[0, :, n] = (np.cos(freqs) * sc)[:, None, None, :]
        tc[1, :, n, :, 0] = (np.sin(freqs) * sc)[:, None, :]
        tc[1, :, n, :, 1] = -(np.sin(freqs) * sc)[:, None, :]
    c["la_tc"] = tc.reshape(2, TILES, P, 2 * P).transpose(2, 0, 1, 3).astype(np.float32)
    return c


def _layout(a):
    import numpy as np

    f = lambda n: np.asarray(a[n])
    cols = lambda *names: np.stack([f(n).reshape(P) for n in names], 1)
    d = {"xT": f("x").reshape(N, P).T}
    tm = "L0_attn_"
    d["tm_vec"] = cols(*(tm + n for n in ("time_maa_x", "time_maa_w", "time_maa_k", "time_maa_v", "time_maa_r", "time_decay",
                                          "time_faaaa", "ln_w", "ln_b")))
    d["tm_w"] = np.concatenate([f(tm + "time_maa_w1"), f(tm + "W_r"), f(tm + "W_k"),
                                f(tm + "W_v"), f(tm + "W_o"), f(tm + "time_decay_w1")], 1)
    w2 = np.zeros((4, 32, 4, P), np.float32)
    for i in range(4):
        w2[i, :, i] = f(tm + "time_maa_w2")[i]
    d["tm_w2"] = w2.reshape(P, 4, P)
    d["tm_dw2"] = f(tm + "time_decay_w2")
    xa = "L0_xattn_"

    def padded(w):
        out = np.zeros((w.shape[0], XH, XPAD), np.float32)
        out[:, :, :XD] = w.reshape(-1, XH, XD)
        return out.reshape(-1, XH * XPAD)

    wp = padded(f(xa + "Wp").T).T.reshape(XH // HG, P, P).transpose(1, 0, 2).reshape(P, -1)
    d["xa_w"] = np.concatenate([f(xa + "Wq"), f(xa + "Wk"), f(xa + "Wcq"), f(xa + "Wv"), wp], 1)
    d["xa_cw"] = np.concatenate([f(xa + "Wck"), f(xa + "Wcv")], 1)
    d["xa_vec"] = cols(*(xa + n for n in ("bq", "bk", "bcq", "bck", "bp")))
    d["xa_vb"] = np.broadcast_to(np.stack([f(xa + n) for n in ("bv", "bcv")]), (P, 2, P))
    ct = f("ctx_512").transpose(2, 0, 1)
    d["ctxT"] = np.concatenate([ct, ct], 2).reshape(CC, B * P)
    la = "L0_ffn_"
    d["la_wqkv"] = f(la + "Wqkv").reshape(DEPTH, P, 3, PAIRS, P).transpose(0, 1, 3, 2, 4).reshape(DEPTH, P, PAIRS, 3 * P)
    d["la_wo"] = f(la + "Wo").reshape(DEPTH, PAIRS, P, P).transpose(0, 2, 1, 3)
    d["la_w1"] = f(la + "W1")
    w2 = np.zeros((DEPTH, len(FC) * P, P), np.float32)
    w2[:, :INNER] = f(la + "W2")
    d["la_w2"] = w2.reshape(DEPTH, len(FC), P, P).transpose(0, 2, 1, 3)
    vec = np.zeros((DEPTH, 8, P), np.float32)
    b1 = f(la + "b1")
    for c, (f0, n) in enumerate(FC):
        vec[:, c, :n], vec[:, 3 + c, :n] = b1[:, f0:f0 + n], b1[:, INNER + f0:INNER + f0 + n]
    vec[:, 6], vec[:, 7] = f(la + "ln_g"), f(la + "ln_b")
    d["la_b2"] = f(la + "b2")[:, :, None]
    d["la_vec"] = vec.transpose(0, 2, 1)
    qk = np.stack([f(la + "q_scale"), f(la + "k_scale")], 1)
    d["la_qks"] = np.broadcast_to(np.concatenate([qk, qk], 2), (P, DEPTH, 2, 2 * LD))
    return d


def kernel(**inputs):
    import numpy as np
    import concourse.bacc as bacc
    from concourse.bass_utils import run_bass_kernel_spmd

    nc = bacc.Bacc("TRN2", target_bir_lowering=False, num_devices=1)
    arrays = {n: np.ascontiguousarray(a) for n, a in {**_layout(inputs), **_constants()}.items()}
    t = {n: nc.dram_tensor(f"in_{n}", a.shape, mybir.dt.from_np(a.dtype), kind="ExternalInput").ap() for n, a in arrays.items()}
    for n in ("identb", "xa_causal", "la_mask"):
        t[n] = t[n].bitcast(BF16)
    t["out"] = nc.dram_tensor("out", (P, N), F32, kind="ExternalOutput").ap()
    build(nc, t)
    r = run_bass_kernel_spmd(nc, [{f"in_{n}": a for n, a in arrays.items()}], core_ids=[0])
    return np.ascontiguousarray(r.results[0]["out"].T).reshape(B, T, P)
```
